# Optimizing a Trainium2 kernel written in Bass

```python
import numpy as np
import jax
import jax.numpy as jnp

def _softmax(x, axis=-1):
    return jax.nn.softmax(x, axis=axis)
def _gelu(x):
    return jax.nn.gelu(x, approximate=True)
def _silu(x):
    return jax.nn.silu(x)
def _sigmoid(x):
    return jax.nn.sigmoid(x)
def _layernorm(x, axis=-1, eps=1e-5):
    m = jnp.mean(x, axis=axis, keepdims=True)
    v = jnp.var(x, axis=axis, keepdims=True)
    return (x - m) / jnp.sqrt(v + eps)
def _scatter_add(tgt, idx, src, axis=0):
    return tgt.at[idx].add(src)
def _segment_sum(src, seg, n):
    return jax.ops.segment_sum(src, seg, n)

kernel_name = 'mk_metaformer_d1_conv_nchw128_debcff'

def setup_inputs(seed: int = 0):
    np.random.seed(seed)
    _w = jnp.asarray
    def _rec_inputs():
        import jax
        import jax.numpy as jnp
        _gk = jax.random.key(seed)
        x = 1.648e-05 + 1 * jax.random.normal(jax.random.fold_in(_gk, 1), (8, 128, 96, 96), jnp.float32)
        return x
    x = _rec_inputs()
    def _L0_conv_setup():
        import jax, jax.numpy as jnp
        import numpy as np
        B, DIM, H, W = (8, 128, 96, 96)
        EPS = 1e-05

        def _mixer(x, W_in, b_in, dw_w, dw_b, gamma, beta, W_out, b_out):
            d = x.shape[-1]
            uv = x @ W_in.T + b_in
            u, v = jnp.split(uv, 2, axis=-1)
            u = jax.nn.silu(u)
            v = jnp.swapaxes(v, 1, 2)
            v = jax.lax.conv_general_dilated(v, dw_w, window_strides=(1,), padding=[(3, 3)], dimension_numbers=('NCH', 'OIH', 'NCH'), feature_group_count=d) + dw_b[None, :, None]
            v = jax.nn.silu(jnp.swapaxes(v, 1, 2))
            y = u * v
            mu = jnp.mean(y, axis=-1, keepdims=True)
            var = jnp.mean((y - mu) ** 2, axis=-1, keepdims=True)
            y = (y - mu) * jax.lax.rsqrt(var + EPS) * gamma + beta
            return y @ W_out.T + b_out
        key = jax.random.key(seed)
        ks = jax.random.split(key, 4)
        d = DIM
        return {'x': jax.random.normal(ks[0], (B, d, H, W), jnp.float32), 'W_in': jax.random.normal(ks[1], (2 * d, d), jnp.float32) * d ** (-0.5), 'b_in': jnp.zeros((2 * d,), jnp.float32), 'dw_w': jax.random.normal(ks[2], (d, 1, 7), jnp.float32) * 0.3, 'dw_b': jnp.zeros((d,), jnp.float32), 'gamma': jnp.ones((d,), jnp.float32), 'beta': jnp.zeros((d,), jnp.float32), 'W_out': jax.random.normal(ks[3], (d, d), jnp.float32) * d ** (-0.5), 'b_out': jnp.zeros((d,), jnp.float32)}
    _L0_conv_all = _L0_conv_setup()
    _L0_conv_in = {k: v for k, v in _L0_conv_all.items() if k in ('W_in', 'b_in', 'dw_w', 'dw_b', 'gamma', 'beta', 'W_out', 'b_out', )}
    del _L0_conv_all

    def _L0_ffn_setup():
        import jax, jax.numpy as jnp
        import numpy as np
        B, N, D, C, E, K = (8, 8192, 128, 128, 8, 2)
        key = jax.random.key(seed)
        k0, k1, k2 = jax.random.split(key, 3)
        x = jax.random.normal(k0, (B, N, D), dtype=jnp.float32)
        router_w = jax.random.normal(k1, (D, E), dtype=jnp.float32) * 0.05
        router_b = jnp.zeros((E,), dtype=jnp.float32)
        expert_w = jax.random.normal(k2, (E, D, C), dtype=jnp.float32) * (1.0 / np.sqrt(D))
        expert_b = jnp.zeros((E, C), dtype=jnp.float32)
        return {'x': x, 'router_w': router_w, 'router_b': router_b, 'expert_w': expert_w, 'expert_b': expert_b}
    _L0_ffn_all = _L0_ffn_setup()
    _L0_ffn_in = {k: v for k, v in _L0_ffn_all.items() if k in ('router_w', 'router_b', 'expert_w', 'expert_b', )}
    del _L0_ffn_all

    return {
        "x": x,
        "L0_conv_W_in": _L0_conv_in["W_in"],
        "L0_conv_b_in": _L0_conv_in["b_in"],
        "L0_conv_dw_w": _L0_conv_in["dw_w"],
        "L0_conv_dw_b": _L0_conv_in["dw_b"],
        "L0_conv_gamma": _L0_conv_in["gamma"],
        "L0_conv_beta": _L0_conv_in["beta"],
        "L0_conv_W_out": _L0_conv_in["W_out"],
        "L0_conv_b_out": _L0_conv_in["b_out"],
        "L0_ffn_router_w": _L0_ffn_in["router_w"],
        "L0_ffn_router_b": _L0_ffn_in["router_b"],
        "L0_ffn_expert_w": _L0_ffn_in["expert_w"],
        "L0_ffn_expert_b": _L0_ffn_in["expert_b"],
    }

def reference(x, L0_conv_W_in, L0_conv_b_in, L0_conv_dw_w, L0_conv_dw_b, L0_conv_gamma, L0_conv_beta, L0_conv_W_out, L0_conv_b_out, L0_ffn_router_w, L0_ffn_router_b, L0_ffn_expert_w, L0_ffn_expert_b):
    import jax
    import jax.numpy as jnp
    def _L0_conv_ref(x, W_in, b_in, dw_w, dw_b, gamma, beta, W_out, b_out):
        import jax, jax.numpy as jnp
        import numpy as np
        B, DIM, H, W = (8, 128, 96, 96)
        EPS = 1e-05

        def _mixer(x, W_in, b_in, dw_w, dw_b, gamma, beta, W_out, b_out):
            d = x.shape[-1]
            uv = x @ W_in.T + b_in
            u, v = jnp.split(uv, 2, axis=-1)
            u = jax.nn.silu(u)
            v = jnp.swapaxes(v, 1, 2)
            v = jax.lax.conv_general_dilated(v, dw_w, window_strides=(1,), padding=[(3, 3)], dimension_numbers=('NCH', 'OIH', 'NCH'), feature_group_count=d) + dw_b[None, :, None]
            v = jax.nn.silu(jnp.swapaxes(v, 1, 2))
            y = u * v
            mu = jnp.mean(y, axis=-1, keepdims=True)
            var = jnp.mean((y - mu) ** 2, axis=-1, keepdims=True)
            y = (y - mu) * jax.lax.rsqrt(var + EPS) * gamma + beta
            return y @ W_out.T + b_out
        Bc, C, Hh, Ww = x.shape
        L = Hh * Ww
        s_lr = jnp.transpose(x, (0, 2, 3, 1)).reshape(Bc, L, C)
        s_tb = jnp.transpose(x, (0, 3, 2, 1)).reshape(Bc, L, C)
        seqs = jnp.concatenate([s_lr, s_tb, s_lr[:, ::-1], s_tb[:, ::-1]], axis=0)
        y = _mixer(seqs, W_in, b_in, dw_w, dw_b, gamma, beta, W_out, b_out)
        y_lr, y_tb, y_rl, y_bt = jnp.split(y, 4, axis=0)
        y_rl = y_rl[:, ::-1]
        y_bt = y_bt[:, ::-1]
        m_lr = jnp.transpose(y_lr.reshape(Bc, Hh, Ww, C), (0, 3, 1, 2))
        m_rl = jnp.transpose(y_rl.reshape(Bc, Hh, Ww, C), (0, 3, 1, 2))
        m_tb = jnp.transpose(y_tb.reshape(Bc, Ww, Hh, C), (0, 3, 2, 1))
        m_bt = jnp.transpose(y_bt.reshape(Bc, Ww, Hh, C), (0, 3, 2, 1))
        return (m_lr + m_tb + m_rl + m_bt) * 0.25

    def _L0_ffn_ref(x, router_w, router_b, expert_w, expert_b):
        import jax, jax.numpy as jnp
        import numpy as np
        B, N, D, C, E, K = (8, 8192, 128, 128, 8, 2)
        router_probs = jax.nn.softmax(x @ router_w + router_b, axis=-1)
        top_p, top_i = jax.lax.top_k(router_probs, K)
        top_p = top_p / jnp.sum(top_p, axis=-1, keepdims=True)
        expert_out = jnp.einsum('bnd,edc->bnec', x, expert_w) + expert_b
        gathered = jnp.take_along_axis(expert_out, top_i[..., None], axis=2)
        return jnp.einsum('bnk,bnkc->bnc', top_p, gathered)

    def _gn(v, G=32, eps=1e-5):
        B_, C_, H_, W_ = v.shape
        g = v.reshape(B_, G, C_ // G, H_, W_)
        m = jnp.mean(g, axis=(2, 3, 4), keepdims=True)
        s = jnp.var(g, axis=(2, 3, 4), keepdims=True)
        return ((g - m) / jnp.sqrt(s + eps)).reshape(v.shape)

    def _ln_c(v, eps=1e-6):
        m = jnp.mean(v, axis=1, keepdims=True)
        s = jnp.var(v, axis=1, keepdims=True)
        return (v - m) / jnp.sqrt(s + eps)

    def _ln_t(v, eps=1e-5):
        m = jnp.mean(v, axis=-1, keepdims=True)
        s = jnp.var(v, axis=-1, keepdims=True)
        return (v - m) / jnp.sqrt(s + eps)

    def _to_tokens(v):
        B_, C_, H_, W_ = v.shape
        return v.reshape(B_, C_, H_ * W_).transpose(0, 2, 1)
    def _from_tokens(t, like):
        B_, C_, H_, W_ = like.shape
        return t.transpose(0, 2, 1).reshape(B_, C_, H_, W_)

    x = x + _L0_conv_ref(_ln_c(x), L0_conv_W_in, L0_conv_b_in, L0_conv_dw_w, L0_conv_dw_b, L0_conv_gamma, L0_conv_beta, L0_conv_W_out, L0_conv_b_out)
    t = _to_tokens(x)
    t = t + _L0_ffn_ref(_ln_t(t), L0_ffn_router_w, L0_ffn_router_b, L0_ffn_expert_w, L0_ffn_expert_b)
    x = _from_tokens(t, x)
    return x


_drawn_inputs = setup_inputs


def setup_inputs(seed=0):
    import zlib

    import numpy as np

    out = dict(_drawn_inputs(seed))
    spreads = {'L0_conv_b_in': (0.0, 0.1),
     'L0_conv_dw_b': (0.0, 0.1),
     'L0_conv_gamma': (1.0, 0.2),
     'L0_conv_beta': (0.0, 0.1),
     'L0_conv_b_out': (0.0, 0.1),
     'L0_ffn_router_b': (0.0, 0.1),
     'L0_ffn_expert_b': (0.0, 0.1)}
    factors = {}
    for name, (base, spread) in spreads.items():
        noise = np.random.default_rng([zlib.crc32(name.encode()), seed]).standard_normal(out[name].shape)
        drawn = base * np.exp(spread * noise) if base else spread * noise
        out[name] = jnp.asarray(drawn.astype(out[name].dtype))
    for name, factor in factors.items():
        out[name] = (out[name] * factor).astype(out[name].dtype)
    return out
```

```python
import concourse.bass as bass
from concourse import mybir
from contextlib import ExitStack

F32 = mybir.dt.float32
BF16 = mybir.dt.bfloat16
ALU = mybir.AluOpType
ACT = mybir.ActivationFunctionType
AX = mybir.AxisListType

B, C, H, W = 8, 128, 96, 96
N = H * W
TAPS = 7
HALO = TAPS // 2
LINE = 96
WIN = LINE + 2 * HALO
KV = WIN + 1
GL = LINE // 2
NG = 4
CH = 4
NCHK = GL // CH
OCT = 8
NOCT = C // OCT
LC = 4
NLC = GL // LC
LN1 = 3 * W
NLN1 = N // LN1
RSTD_ROWS = 3 * 32
START = 1
EPS_LNC, EPS_MIX, EPS_TOK = 1e-6, 1e-5, 1e-5
E = 8
TB = 4 * W
NTB = N // TB
TT = N // 128
TPC = TB // 128


def build(nc, x, w_in, b_in, dw_w, dw_b, gamma, beta, w_out, b_out, router_w, router_b, expert_w, expert_b, out):
    x_v = x.rearrange("b c h w -> b c (h w)")
    out_v = out.rearrange("b c h w -> b c (h w)")
    z_rows = nc.dram_tensor("z_rows", [B, C, N], F32).ap()
    z_cols = nc.dram_tensor("z_cols", [B, C, N], F32).ap()

    top = ExitStack()
    with top:
        def keep(name, shape, dt=F32):
            return top.enter_context(nc.sbuf_tensor(name, shape, dt))

        ident = keep("ident", [128, 128])
        mean_w = keep("mean_w", [128, 128])
        mhalf = keep("mhalf", [128, 1])
        var_sel = keep("var_sel", [128, 31 + RSTD_ROWS])
        row_sel = keep("row_sel", [RSTD_ROWS, 32], BF16)
        wout_hi = keep("wout_hi", [128, 128], BF16)
        wout_lo = keep("wout_lo", [128, 128], BF16)
        proj_b = keep("proj_b", [128, 1])
        psum = [top.enter_context(nc.psum_tensor(f"bank{i}", [128, 512], F32)) for i in range(4)]
        pairs = [top.enter_context(nc.psum_tensor(f"pair{i}", [128, 2, 512], F32)) for i in range(2)]

        mixer(nc, locals())
        experts(nc, locals())


def rstd_rows(nc, dve, i, vr, vparts, var, eps, s_ln, s_inv, s_sqrt, s_root):
    step = [0]

    def link(ins):
        step[0] += 1
        ins.then_inc(s_ln, 1)
        dve.wait_ge(s_ln, i * LN_CHAIN + step[0])
    link(nc.vector.tensor_scalar(vr[:, 0, :], var, eps, None, ALU.add))
    nc.vector.reciprocal(vr[:, 1, :], vr[:, 0, :]).then_inc(s_inv, 1)
    dve.wait_ge(s_sqrt, i + 1)
    link(nc.vector.tensor_tensor(vr[:, 3, :], vr[:, 2, :], vr[:, 2, :], ALU.mult))
    link(nc.vector.tensor_tensor(vr[:, 3, :], vr[:, 3, :], vr[:, 0, :], ALU.mult))
    link(nc.vector.tensor_scalar(vr[:, 3, :], vr[:, 3, :], -0.5, 1.5, ALU.mult, ALU.add))
    link(nc.vector.tensor_tensor(vr[:, 3, :], vr[:, 3, :], vr[:, 2, :], ALU.mult))
    link(nc.vector.tensor_copy(vparts, vr[:, 3, :]))
    link(nc.vector.tensor_tensor(vr[:, 0, :], vr[:, 3, :], vparts, ALU.subtract))
    nc.vector.tensor_copy(vparts[32:64, :], vr[32:64, 0, :])
    link(nc.vector.tensor_copy(vparts[64:96, :], vr[64:96, 0, :]))
    link(nc.vector.tensor_tensor(vr[64:96, 1, :], vr[64:96, 0, :], vparts[64:96, :], ALU.subtract))
    nc.vector.tensor_copy(vparts[64:96, :], vr[64:96, 1, :]).then_inc(s_root, 1)


LN_CHAIN = 9


def mixer(nc, g):
    x_v, z_rows, z_cols = g["x_v"], g["z_rows"], g["z_cols"]
    ident, mean_w, mhalf, var_sel, row_sel = g["ident"], g["mean_w"], g["mhalf"], g["var_sel"], g["row_sel"]
    wout_hi, wout_lo, proj_b = g["wout_hi"], g["wout_lo"], g["proj_b"]
    vbank, ubank, pair = g["psum"][0:2], g["psum"][2:4], g["pairs"]
    ctx = ExitStack()
    with ctx:
        def sb(name, shape, dt=F32):
            return ctx.enter_context(nc.sbuf_tensor(name, shape, dt))

        def sem(name):
            return ctx.enter_context(nc.semaphore(name))

        TL, HL = LINE * 2 * C, (H + 2 * HALO) * W
        t_h = sb("t_h", [128, 2 * TL + HL], BF16)
        t_lo = t_h[:, 0:TL].rearrange("p (m d c) -> p m d c", m=LINE, d=2)
        t_hi = t_h[:, TL:2 * TL].rearrange("p (m d c) -> p m d c", m=LINE, d=2)
        h_hi = t_h[:, 2 * TL:].rearrange("p (r w) -> p r w", w=W)
        bufs = sb("bufs", [128, 2, C, GL])
        buf_b = bufs[:, 0, :, :]
        y_f = bufs[:, 1, :, :]
        buf_a = y_f.rearrange("p c g -> p (c g)").bitcast(BF16).rearrange("p (c g t) -> p c g t", c=C, t=2)
        xc = bufs[:, :, :, :].rearrange("p s c g -> p (s c g)")[:, 0:N]
        OVER = -(-(N - C * GL) // GL)
        h_lo = sb("h_lo", [128, H + 2 * HALO, W], BF16)
        sq = sb("sq", [128, 2, LN1])
        hf = sb("hf", [128, 2, LN1])
        sv = sb("sv", [128, 2, 2, OCT * GL])
        sv_flat = sv[0:RSTD_ROWS, :, :, :].rearrange("p a b n -> p (a b n)")
        vr = sv_flat[:, 0:4 * LN1].rearrange("p (k n) -> p k n", k=4)
        vparts = sv_flat[:, 4 * LN1:4 * LN1 + LN1 // 2].bitcast(BF16)
        zt = sb("zt", [128, 2, CH * LINE])
        win_hi = sb("win_hi", [128, 2, C], BF16)
        win_lo = sb("win_lo", [128, 2, C], BF16)
        stats = sb("stats", [128, LC, 2, 6])
        st = sb("st", [128, 7, LC, 2])
        rstd = sb("rstd", [128, 2, LC, 2])
        ones3 = sb("ones3", [3, 128], BF16)
        bu3 = sb("bu3", [3, CH, C], BF16)
        negbv = sb("negbv", [1, C])
        edge = sb("edge", [1, 2, 128])

        s_load = sem("weights_loaded")
        s_pc = sem("pool_constants")
        s_dv = sem("dve_step")
        s_ac = sem("act_step")
        s_pe = sem("pe_step")
        s_ready = sem("mixer_weights_ready")

        wctx = ExitStack()
        with wctx:
            def ws(name, shape, dt=F32):
                return wctx.enter_context(nc.sbuf_tensor(name, shape, dt))
            win_n = buf_b[:, 0:6, :].rearrange("p c g -> p (c g)")[:, 0:2 * C].rearrange("p (s d) -> p s d", s=2)
            wout_n = buf_b[:, 6:9, :].rearrange("p c g -> p (c g)")[:, 0:C]
            wf = buf_b[:, 9:15, :].rearrange("p c g -> p (c g)")[:, 0:2 * C].rearrange("p (s d) -> p s d", s=2)
            wof = buf_b[:, 15:18, :].rearrange("p c g -> p (c g)")[:, 0:C]
            dwn = buf_b[:, 18, 0:TAPS]
            dwr = buf_b[:, 19, 0:TAPS]
            cols = buf_b[:, 20, 0:6]
            tmp = buf_b[:, 21, 0:2]
            taps = buf_b[0:TAPS, 22:28, :].rearrange("p c g -> p (c g)")[:, 0:2 * C]
            cb_row = buf_b[0:1, 28:34, :].rearrange("p c g -> p (c g)")[:, 0:2 * C]
            bu_row = buf_b[0:1, 34:37, :].rearrange("p c g -> p (c g)")[:, 0:C]
            bu_res = buf_b[0:1, 37:40, :].rearrange("p c g -> p (c g)")[:, 0:C]
            zband = buf_b[0:TAPS, 40:46, :].rearrange("p c g -> p (c g)")[:, 0:LINE - 1 + KV]
            last = buf_b[0:1, 46:49, :].rearrange("p c g -> p (c g)")[:, 0:KV]
            bu_part = buf_b[0:1, 49:58, :].rearrange("p c g -> p (c g)").bitcast(BF16)[:, 0:3 * C]\
                .rearrange("p (k c) -> p k c", k=3)
            bv_row = buf_b[0:1, 58:61, :].rearrange("p c g -> p (c g)")[:, 0:C]

            with nc.Block() as block:
                @block.sync
                def _(sp):
                    sp.dma_start(win_n[:, :, :], g["w_in"].rearrange("(s o) d -> o s d", s=2)).then_inc(s_load, 16)
                    sp.dma_start(wout_n, g["w_out"]).then_inc(s_load, 16)
                    sp.dma_start(dwn, g["dw_w"].rearrange("c a k -> c (a k)")).then_inc(s_load, 16)
                    sp.dma_start(cols[:, 0:1], g["b_in"].rearrange("(s c a) -> s c a", s=2, a=1)[1]).then_inc(s_load, 16)
                    for n, v in enumerate(("dw_b", "gamma", "beta", "b_out")):
                        sp.dma_start(cols[:, n + 1:n + 2], g[v].rearrange("(c a) -> c a", a=1)).then_inc(s_load, 16)
                    sp.dma_start(bu_row, g["b_in"].rearrange("(s c) -> s c", s=2)[0:1]).then_inc(s_load, 16)
                    sp.dma_start(bv_row, g["b_in"].rearrange("(s c) -> s c", s=2)[1:2]).then_inc(s_load, 16)
                    sp.wait_ge(s_dv, BU_PARTS)
                    for k in range(3):
                        for j in range(CH):
                            sp.dma_start(bu3[k:k + 1, j, :], bu_part[:, k, :]).then_inc(s_load, 16)
                    sp.wait_ge(s_load, 16 * (10 + 3 * CH))

                @block.gpsimd
                def _(pool):
                    step = [0]

                    def done(ins):
                        step[0] += 1
                        ins.then_inc(s_pc, 1)
                        pool.wait_ge(s_pc, step[0])
                    done(nc.gpsimd.memset(ident[:, :], 0.0))
                    done(nc.gpsimd.affine_select(out=ident[:, :], in_=ident[:, :], compare_op=ALU.not_equal, fill=1.0,
                                                 base=0, pattern=[[-1, 128]], channel_multiplier=1))
                    done(nc.gpsimd.memset(mean_w[:, :], 1.0 / C))
                    done(nc.gpsimd.memset(mhalf[:, :], -0.5))
                    done(nc.gpsimd.memset(var_sel[:, :], 0.0))
                    done(nc.gpsimd.memset(var_sel[:, 31:31 + RSTD_ROWS:32], 1.0 / C))
                    done(nc.gpsimd.memset(row_sel[:, :], 0.0))
                    for k in range(3):
                        done(nc.gpsimd.affine_select(out=row_sel[:, :], in_=row_sel[:, :], compare_op=ALU.not_equal, fill=1.0,
                                                     base=-32 * k, pattern=[[-1, 32]], channel_multiplier=1))
                    done(nc.gpsimd.memset(zband, 0.0))
                    done(nc.gpsimd.affine_select(out=zband, in_=zband, compare_op=ALU.not_equal, fill=1.0,
                                                 base=LINE - 1, pattern=[[-1, LINE - 1 + KV]], channel_multiplier=1))
                    done(nc.gpsimd.memset(last, 0.0))
                    done(nc.gpsimd.memset(last[:, WIN:KV], 1.0))
                    done(nc.gpsimd.memset(ones3[:, :], 1.0))
                    done(nc.gpsimd.memset(edge[:, :, :], 0.0))
                    done(nc.gpsimd.memset(edge[:, 0, 0:HALO], 1.0))
                    done(nc.gpsimd.memset(edge[:, 1, WIN - HALO:WIN], 1.0))
                    done(nc.gpsimd.memset(h_hi[:, :, :], 0.0))
                    done(nc.gpsimd.memset(h_lo[:, :, :], 0.0))
                    done(nc.gpsimd.memset(buf_a[:, :, :, 0], 1.0))
                    done(nc.gpsimd.memset(buf_a[:, :, :, 1], 0.0))
                    assert step[0] == POOL_CONSTS

                @block.vector
                def _(dve):
                    step = [0]

                    def done(ins):
                        step[0] += 1
                        ins.then_inc(s_dv, 1)
                        dve.wait_ge(s_dv, step[0])
                    dve.wait_ge(s_load, 16 * 10)
                    done(nc.vector.tensor_copy(bu_part[:, 0, :], bu_row))
                    done(nc.vector.tensor_tensor(bu_res, bu_row, bu_part[:, 0, :], ALU.subtract))
                    done(nc.vector.tensor_copy(bu_part[:, 1, :], bu_res))
                    done(nc.vector.tensor_tensor(bu_row, bu_res, bu_part[:, 1, :], ALU.subtract))
                    done(nc.vector.tensor_copy(bu_part[:, 2, :], bu_row))
                    assert step[0] == BU_PARTS
                    done(nc.vector.tensor_scalar(negbv[:, :], bv_row, -1.0, None, ALU.mult))
                    for j in range(TAPS):
                        done(nc.vector.tensor_copy(dwr[:, j:j + 1], dwn[:, TAPS - 1 - j:TAPS - j]))
                    done(nc.vector.reduce_sum(tmp[:, 0:1], dwn, AX.X))
                    done(nc.vector.tensor_scalar(tmp[:, 1:2], tmp[:, 0:1], cols[:, 0:1], cols[:, 1:2], ALU.mult, ALU.add))
                    assert step[0] == DVE_NATURAL
                    dve.wait_ge(s_pe, 1)
                    done(nc.vector.tensor_copy(wf[:, :, :], vbank[0][:, 0:2 * C].rearrange("p (s d) -> p s d", s=2)))
                    done(nc.vector.tensor_copy(win_hi[:, :, :], wf[:, :, :]))
                    done(nc.vector.tensor_tensor(win_lo[:, :, :], wf[:, :, :], win_hi[:, :, :], ALU.subtract))
                    done(nc.vector.tensor_copy(wof, vbank[1][:, 0:C]))
                    done(nc.vector.tensor_copy(taps, ubank[0][0:TAPS, 0:2 * C]))
                    done(nc.vector.tensor_copy(cb_row[:, 0:C], ubank[1][0:1, 0:C]))
                    done(nc.vector.tensor_copy(cb_row[:, C:2 * C], ubank[1][0:1, 0:C]))
                    assert step[0] == DVE_EVAC
                    dve.wait_ge(s_pe, 2)
                    done(nc.vector.tensor_tensor(proj_b[:, :], vbank[0][:, 0:1], cols[:, 4:5], ALU.add))
                    done(nc.vector.tensor_scalar(wof, wof, cols[:, 2:3], 0.25, ALU.mult, ALU.mult))
                    dve.wait_ge(s_pe, 3)
                    done(nc.vector.tensor_tensor(wof, wof, vbank[1][:, 0:C], ALU.subtract))
                    done(nc.vector.tensor_copy(wout_hi[:, :], wof))
                    done(nc.vector.tensor_tensor(wout_lo[:, :], wof, wout_hi[:, :], ALU.subtract))
                    for n in range(LINE // 2):
                        dve.wait_ge(s_ac, n + 1)
                        nc.vector.tensor_tensor(
                            t_lo[0:KV, 2 * n:2 * n + 2, :, :].rearrange("p m d c -> p (m d c)"), pair[n % 2][0:KV, 0, :],
                            t_hi[0:KV, 2 * n:2 * n + 2, :, :].rearrange("p m d c -> p (m d c)"),
                            ALU.subtract).then_inc(s_ready, 1)
                    dve.wait_ge(s_ready, LINE // 2)

                @block.scalar
                def _(act):
                    for n in range(LINE // 2):
                        act.wait_ge(s_pe, 4 + n)
                        nc.scalar.activation(t_hi[0:KV, 2 * n:2 * n + 2, :, :].rearrange("p m d c -> p (m d c)"),
                                             pair[n % 2][0:KV, 0, :], ACT.Copy).then_inc(s_ac, 1)
                    act.wait_ge(s_ac, LINE // 2)

                @block.tensor
                def _(pe):
                    pe.wait_ge(s_load, 16 * 10)
                    pe.wait_ge(s_pc, POOL_CONSTS)
                    pe.wait_ge(s_dv, DVE_NATURAL)
                    for n, s in enumerate((1, 0)):
                        nc.tensor.matmul(vbank[0][:, n * C:(n + 1) * C], win_n[:, s, :], ident[:, :], start=True, stop=True)
                    nc.tensor.matmul(vbank[1][:, 0:C], wout_n, ident[:, :], start=True, stop=True)
                    nc.tensor.matmul(ubank[0][0:TAPS, 0:C], dwn, ident[:, :], start=True, stop=True)
                    nc.tensor.matmul(ubank[0][0:TAPS, C:2 * C], dwr, ident[:, :], start=True, stop=True)
                    nc.tensor.matmul(ubank[1][0:1, 0:C], tmp[:, 1:2], ident[:, :], start=True, stop=True).then_inc(s_pe, 1)
                    pe.wait_ge(s_dv, DVE_EVAC)
                    nc.tensor.matmul(vbank[0][:, 0:1], wof, cols[:, 3:4], start=True, stop=True).then_inc(s_pe, 1)
                    pe.wait_ge(s_dv, DVE_EVAC + 2)
                    nc.tensor.matmul(vbank[1][:, 0:C], mean_w[:, :], wof, start=True, stop=True).then_inc(s_pe, 1)
                    for n in range(LINE // 2):
                        if n >= 2:
                            pe.wait_ge(s_ready, n - 1)
                        for j in range(2):
                            m = 2 * n + j
                            o = pair[n % 2][0:KV, 0, j * 2 * C:(j + 1) * 2 * C]
                            nc.tensor.matmul(o, zband[:, LINE - 1 - m:LINE - 1 - m + KV], taps, start=True, stop=False)
                            mm = nc.tensor.matmul(o, last, cb_row, start=False, stop=True)
                        mm.then_inc(s_pe, 1)

        XL = 8
        s_x = [sem(f"x_part_loaded_{n}") for n in range(XL)]
        s_mean = sem("mean_done")
        s_xc = sem("x_centred")
        s_sq = sem("x_squared")
        s_var = sem("var_done")
        s_root = sem("image_rstd_done")
        s_inv = sem("inverse_variance_done")
        s_sqrt = sem("root_done")
        s_ln = sem("rstd_chain")
        s_bc = sem("rstd_broadcast")
        s_one = sem("bias_row_restored")
        s_hf = sem("h_done")
        s_hh = sem("h_high_done")
        s_hl = sem("h_low_done")
        s_halo = sem("halo_rows_done")
        s_v = sem("v_product_done")
        s_u = sem("u_product_done")
        s_vh = sem("v_high_done")
        s_vl = sem("v_low_done")
        s_su = sem("silu_u_done")
        s_conv = sem("conv_done")
        s_sv = sem("silu_conv_done")
        s_yf = sem("y_forward_done")
        s_yr = sem("y_reversed_done")
        s_ch = sem("dve_chain")
        s_mv = sem("variances_ready")
        s_r = sem("line_rstd_ready")
        s_sc = sem("y_forward_scaled")
        s_sb = sem("y_reversed_scaled")
        s_z = sem("z_lines_done")
        s_tr = sem("z_transposed")
        s_zt = sem("z_copied")
        s_zst = [sem(f"z_stored_{i}") for i in range(2)]

        from_one = (s_xc, s_vl, s_su, s_zt, s_var, s_yr, s_zst[0], s_zst[1], s_hl)
        UV = NG * NCHK
        CV = NG * NOCT

        with nc.Block() as block:
            @block.sync
            def _(sp):
                with sp.Fori(0, B) as i:
                    sp.wait_ge(s_zt, START + i * UV)
                    for n in range(XL):
                        sp.dma_start(xc[:, n * (N // XL):(n + 1) * (N // XL)],
                                     x_v[bass.ds(i, 1), :, n * (N // XL):(n + 1) * (N // XL)].rearrange("b c n -> (b c) n")
                                     ).then_inc(s_x[n], 16)
                    for k in range(UV):
                        sp.wait_ge(s_zt, START + i * UV + k + 1)
                        dst = z_rows if k < UV // 2 else z_cols
                        kk = k % (UV // 2)
                        sp.dma_start(dst[bass.ds(i, 1), :, kk * CH * LINE:(kk + 1) * CH * LINE].rearrange("b c n -> (b c) n"),
                                     zt[:, k % 2, :]).then_inc(s_zst[k % 2], 16)
                for p in range(2):
                    sp.wait_ge(s_zst[p], START + 16 * B * UV // 2)

            @block.tensor
            def _(pe):
                with pe.Fori(0, B) as i:
                    def mean(n):
                        pe.wait_ge(s_x[n * XL // NLN1], i * 16 + 16)
                        if n >= 2:
                            pe.wait_ge(s_xc, START + i * NLN1 + n - 1)
                        else:
                            pe.wait_ge(s_vl, START + i * UV)
                        nc.tensor.matmul(vbank[n % 2][:, 0:LN1], mean_w[:, :], xc[:, n * LN1:(n + 1) * LN1], start=True, stop=True
                                         ).then_inc(s_mean, 1)

                    def var(n):
                        pe.wait_ge(s_sq, i * NLN1 + n + 1)
                        if n == 0:
                            pe.wait_ge(s_su, START + i * UV)
                        nc.tensor.matmul(ubank[0][0:RSTD_ROWS, 0:LN1], var_sel[:, 31 - n:31 - n + RSTD_ROWS], sq[:, n % 2, :],
                                         start=(n == 0), stop=(n == NLN1 - 1)).then_inc(s_var, 1)

                    def spread(n):
                        if n >= 2:
                            pe.wait_ge(s_hf, i * NLN1 + n - 1)
                        else:
                            pe.wait_ge(s_root, i + 1)
                        nc.tensor.matmul(vbank[n % 2][:, 0:LN1], row_sel[:, n:n + 1].to_broadcast([RSTD_ROWS, 128]), vparts,
                                         start=True, stop=True).then_inc(s_bc, 1)

                    for n in range(NLN1):
                        mean(n)
                        if n >= 1:
                            var(n - 1)
                    var(NLN1 - 1)
                    for n in range(NLN1):
                        spread(n)

                    def window(h, line, cols, lo, cnt):
                        if cols:
                            return h[:, lo:lo + cnt, line]
                        flat = h[:, :, :].rearrange("p r w -> p (r w)")
                        at = (line + HALO) * W - HALO + lo
                        return flat[:, at:at + cnt]

                    def uv(k):
                        grp, ch = divmod(k, NCHK)
                        cols = grp >= 2
                        l0 = (grp % 2) * GL + ch * CH
                        vb, ub = vbank[k % 2], ubank[k % 2]
                        if k >= 2:
                            pe.wait_ge(s_vl, START + i * UV + k - 1)
                            pe.wait_ge(s_su, START + i * UV + k - 1)
                        else:
                            pe.wait_ge(s_hf, (i + 1) * NLN1)
                        nc.tensor.matmul(ub[0:LINE, :], ones3[:, 0:LINE], bu3[:, :, :].rearrange("p j c -> p (j c)"),
                                         start=True, stop=False, skip_group_check=True)
                        for j in range(CH):
                            o = ub[0:LINE, j * C:(j + 1) * C]
                            for n, (hh, ww) in enumerate(((h_hi, win_hi), (h_hi, win_lo), (h_lo, win_hi))):
                                mm = nc.tensor.matmul(o, window(hh, l0 + j, cols, HALO, LINE), ww[:, 1, :],
                                                      start=False, stop=(n == 2), skip_group_check=True)
                        mm.then_inc(s_u, 1)
                        for j in range(CH):
                            o = vb[0:WIN, j * C:(j + 1) * C]
                            at_edge = (l0 + j) in (0, LINE - 1)
                            first = [j == 0]
                            if at_edge:
                                s = 0 if l0 + j == 0 else 1
                                nc.tensor.matmul(o, edge[:, s, 0:WIN], negbv[:, :], start=first[0], stop=False,
                                                 skip_group_check=True)
                                first[0] = False
                            for n, (hh, ww) in enumerate(((h_hi, win_hi), (h_hi, win_lo), (h_lo, win_hi))):
                                mm = nc.tensor.matmul(o, window(hh, l0 + j, cols, 0, WIN), ww[:, 0, :],
                                                      start=first[0], stop=(n == 2), skip_group_check=True)
                                first[0] = False
                        mm.then_inc(s_v, 1)

                    def conv(q):
                        o8 = (q % NOCT) * OCT
                        if q % NOCT == 0:
                            pe.wait_ge(s_vl, START + i * UV + (q // NOCT + 1) * NCHK)
                            pe.wait_ge(s_zt, START + i * UV + q // NOCT * NCHK)
                        if q % NOCT >= 2:
                            pe.wait_ge(s_sv, i * CV + q - 1)
                        for d in range(2):
                            for c in range(OCT):
                                o = pair[q % 2][:, d, c * GL:(c + 1) * GL]
                                ops = ((TL, 0), (0, 0), (TL, 1))
                                for n, (at, part) in enumerate(ops):
                                    at += d * C + o8 + c
                                    mm = nc.tensor.matmul(o, t_h[0:KV, at:at + 127 * 2 * C + 1:2 * C],
                                                          buf_a[0:KV, o8 + c, :, part],
                                                          start=(c == 0 and n == 0), stop=(n == 2), skip_group_check=True)
                        mm.then_inc(s_conv, 1)

                    def turn(k):
                        grp, ch = divmod(k, NCHK)
                        pe.wait_ge(s_z, i * NG * NLC + grp * NLC + ch * CH // LC + 1)
                        if ch >= 2:
                            pe.wait_ge(s_zt, START + i * UV + k - 1)
                        else:
                            pe.wait_ge(s_sv, i * CV + (grp + 1) * NOCT)
                        for j in range(CH):
                            mm = nc.tensor.transpose(pair[k % 2][:, 0, j * LINE:(j + 1) * LINE],
                                                     y_f[0:LINE, :, ch * CH + j], ident[0:LINE, 0:LINE])
                        mm.then_inc(s_tr, 1)

                    pe.wait_ge(s_hl, START + (i + 1) * NLN1)
                    for k in range(NCHK):
                        uv(k)
                    for grp in range(NG):
                        if grp == 1:
                            pe.wait_ge(s_halo, (i + 1) * 4)
                        for q in range(grp * NOCT, (grp + 1) * NOCT):
                            conv(q)
                        for k in range(grp * NCHK, (grp + 1) * NCHK):
                            turn(k)
                            if grp < NG - 1:
                                uv(k + NCHK)

            @block.scalar
            def _(act):
                with act.Fori(0, B) as i:
                    def square(n):
                        act.wait_ge(s_xc, START + i * NLN1 + n + 1)
                        act.wait_ge(s_var, START + i * NLN1 + max(n - 1, 0))
                        nc.scalar.activation(sq[:, n % 2, :], xc[:, n * LN1:(n + 1) * LN1], ACT.Square).then_inc(s_sq, 1)

                    def high(n):
                        act.wait_ge(s_hf, i * NLN1 + n + 1)
                        r0 = HALO + n * (LN1 // W)
                        nc.scalar.activation(h_hi[:, r0:r0 + LN1 // W, :].rearrange("p r w -> p (r w)"), hf[:, n % 2, :],
                                             ACT.Copy).then_inc(s_hh, 1)

                    for n in range(NLN1):
                        square(n)
                    act.wait_ge(s_inv, i + 1)
                    nc.scalar.activation(vr[:, 2, :], vr[:, 1, :], ACT.Sqrt).then_inc(s_sqrt, 1)
                    for n in range(NLN1):
                        high(n)

                    def uv_out(k):
                        grp, ch = divmod(k, NCHK)
                        ls = slice(ch * CH, (ch + 1) * CH)
                        act.wait_ge(s_u, i * UV + k + 1)
                        nc.scalar.activation(buf_b[0:LINE, :, ls].rearrange("p c g -> p g c"),
                                             ubank[k % 2][0:LINE, :].rearrange("p (g c) -> p g c", g=CH), ACT.Silu
                                             ).then_inc(s_su, 1)
                        act.wait_ge(s_v, i * UV + k + 1)
                        if k == 0:
                            act.wait_ge(s_one, i + 1)
                        nc.scalar.activation(buf_a[0:WIN, :, ls, 0].rearrange("p c g -> p g c"),
                                             vbank[k % 2][0:WIN, :].rearrange("p (g c) -> p g c", g=CH), ACT.Copy
                                             ).then_inc(s_vh, 1)

                    for k in range(NCHK):
                        uv_out(k)
                    for grp in range(NG):
                        for q in range(grp * NOCT, (grp + 1) * NOCT):
                            act.wait_ge(s_conv, i * CV + q + 1)
                            act.wait_ge(s_yr, START + i * CV + max(q - 1, 0))
                            nc.scalar.activation(sv[0:LINE, q % 2, :, :], pair[q % 2][0:LINE, :, 0:OCT * GL], ACT.Silu
                                                 ).then_inc(s_sv, 1)
                        def scale_reversed(c):
                            act.wait_ge(s_r, i * NG * NLC + grp * NLC + c + 1)
                            for l in range(LC):
                                y = buf_b[0:LINE, :, c * LC + l]
                                last = nc.scalar.activation(y, y, ACT.Copy, scale=rstd[0:LINE, c % 2, l, 1:2])
                            last.then_inc(s_sb, 1)

                        scale_reversed(0)
                        for k in range(grp * NCHK, (grp + 1) * NCHK):
                            if k % NCHK + 1 < NLC:
                                scale_reversed(k % NCHK + 1)
                            act.wait_ge(s_tr, i * UV + k + 1)
                            act.wait_ge(s_zst[k % 2], START + i * (16 * (UV // 2)) + 16 * (k // 2))
                            nc.scalar.activation(zt[:, k % 2, :], pair[k % 2][:, 0, 0:CH * LINE], ACT.Copy).then_inc(s_zt, 1)
                            if grp < NG - 1:
                                uv_out(k + NCHK)
                        if grp == 0:
                            for h in (h_hi, h_lo):
                                nc.scalar.activation(h[:, 0:HALO, 1:W], h[:, H:H + HALO, 0:W - 1], ACT.Copy).then_inc(s_halo, 1)
                                nc.scalar.activation(h[:, H + HALO:H + 2 * HALO, 0:W - 1], h[:, HALO:2 * HALO, 1:W],
                                                     ACT.Copy).then_inc(s_halo, 1)

            @block.gpsimd
            def _(pool):
                for s in from_one:
                    pool.sem_inc(s, START)
                with pool.Fori(0, B) as i:
                    def low(n):
                        pool.wait_ge(s_hh, i * NLN1 + n + 1)
                        r0 = HALO + n * (LN1 // W)
                        o = (slice(None), slice(r0, r0 + LN1 // W), slice(None))
                        nc.gpsimd.tensor_tensor(h_lo[o].rearrange("p r w -> p (r w)"), hf[:, n % 2, :],
                                                h_hi[o].rearrange("p r w -> p (r w)"), ALU.subtract).then_inc(s_hl, 1)

                    for h in (h_hi, h_lo):
                        nc.gpsimd.memset(h[:, HALO - 1, W - HALO:W], 0.0)
                        nc.gpsimd.memset(h[:, H + HALO, 0:HALO], 0.0)
                    for n in range(NLN1):
                        low(n)

                    for grp in range(NG):
                        for q in range(grp * NOCT, (grp + 1) * NOCT):
                            o8 = (q % NOCT) * OCT
                            pool.wait_ge(s_sv, i * CV + q + 1)
                            nc.gpsimd.tensor_tensor(y_f[0:LINE, o8:o8 + OCT, :].rearrange("p c g -> p (c g)"),
                                                    buf_b[0:LINE, o8:o8 + OCT, :].rearrange("p c g -> p (c g)"),
                                                    sv[0:LINE, q % 2, 0, :], ALU.mult).then_inc(s_yf, 1)
                        for c in range(NLC):
                            pool.wait_ge(s_mv, i * NG * NLC + grp * NLC + c + 1)
                            nc.gpsimd.tensor_tensor(rstd[0:LINE, c % 2, :, :], st[0:LINE, 5 + c % 2, :, :],
                                                    mhalf[0:LINE, 0:1].unsqueeze(2).to_broadcast([LINE, LC, 2]), ALU.pow
                                                    ).then_inc(s_r, 1)
                            pool.wait_ge(s_r, i * NG * NLC + grp * NLC + c + 1)
                            y = y_f[0:LINE, :, c * LC:(c + 1) * LC]
                            nc.gpsimd.tensor_tensor(y, y, rstd[0:LINE, c % 2, :, 0].unsqueeze(1).to_broadcast([LINE, C, LC]),
                                                    ALU.mult).then_inc(s_sc, 1)

            @block.vector
            def _(dve):
                with dve.Fori(0, B) as i:
                    CHAIN = NG * NLC * CHAIN_PER_CHUNK
                    chain = [0]

                    def link(ins):
                        chain[0] += 1
                        ins.then_inc(s_ch, 1)
                        dve.wait_ge(s_ch, i * CHAIN + chain[0])

                    def centre(n):
                        dve.wait_ge(s_mean, i * NLN1 + n + 1)
                        v = xc[:, n * LN1:(n + 1) * LN1]
                        nc.vector.tensor_tensor(v, v, vbank[n % 2][:, 0:LN1], ALU.subtract).then_inc(s_xc, 1)

                    def normal(n):
                        dve.wait_ge(s_bc, i * NLN1 + n + 1)
                        dve.wait_ge(s_hl, START + i * NLN1 + max(n - 1, 0))
                        nc.vector.tensor_tensor(hf[:, n % 2, :], xc[:, n * LN1:(n + 1) * LN1], vbank[n % 2][:, 0:LN1],
                                                ALU.mult).then_inc(s_hf, 1)

                    for n in range(NLN1):
                        centre(n)
                    dve.wait_ge(s_var, START + (i + 1) * NLN1)
                    rstd_rows(nc, dve, i, vr, vparts, ubank[0][0:RSTD_ROWS, 0:LN1], EPS_LNC, s_ln, s_inv, s_sqrt, s_root)
                    for n in range(NLN1):
                        normal(n)
                    dve.wait_ge(s_hf, (i + 1) * NLN1)
                    nc.vector.memset(y_f[96:128, 0:OVER, :].rearrange("p c g -> p (c g)").bitcast(mybir.dt.uint32), 0x3F80
                                     ).then_inc(s_one, 1)

                    def v_low(k):
                        grp, ch = divmod(k, NCHK)
                        ls = slice(ch * CH, (ch + 1) * CH)
                        dve.wait_ge(s_vh, i * UV + k + 1)
                        nc.vector.tensor_tensor(buf_a[0:WIN, :, ls, 1].rearrange("p c g -> p g c"),
                                                vbank[k % 2][0:WIN, :].rearrange("p (g c) -> p g c", g=CH),
                                                buf_a[0:WIN, :, ls, 0].rearrange("p c g -> p g c"), ALU.subtract
                                                ).then_inc(s_vl, 1)

                    def line_stats(grp, c):
                        for l in range(LC):
                            for d, y in enumerate((y_f, buf_b)):
                                ins = nc.vector.bn_stats(stats[0:LINE, l, d, :], y[0:LINE, :, c * LC + l])
                        link(ins)
                        s = [stats[0:LINE, :, :, n] for n in range(6)]
                        nc.vector.tensor_tensor(st[0:LINE, 0, :, :], s[1], s[4], ALU.subtract)
                        link(nc.vector.tensor_tensor(st[0:LINE, 1, :, :], s[2], s[5], ALU.add))
                        link(nc.vector.tensor_tensor(st[0:LINE, 2, :, :], st[0:LINE, 0, :, :], st[0:LINE, 0, :, :], ALU.mult))
                        link(nc.vector.scalar_tensor_tensor(out=st[0:LINE, 3, :, :], in0=st[0:LINE, 2, :, :],
                                                            scalar=C / 4.0, in1=st[0:LINE, 1, :, :],
                                                            op0=ALU.mult, op1=ALU.add))
                        nc.vector.tensor_scalar(st[0:LINE, 5 + c % 2, :, :], st[0:LINE, 3, :, :], 1.0 / C, EPS_MIX,
                                                ALU.mult, ALU.add).then_inc(s_mv, 1)

                    def lines_out(grp, c):
                        dve.wait_ge(s_sc, i * NG * NLC + grp * NLC + c + 1)
                        dve.wait_ge(s_sb, i * NG * NLC + grp * NLC + c + 1)
                        y = y_f[0:LINE, :, c * LC:(c + 1) * LC]
                        last = nc.vector.tensor_tensor(y, y, buf_b[0:LINE, :, c * LC:(c + 1) * LC], ALU.add)
                        last.then_inc(s_z, 1)

                    for k in range(NCHK):
                        v_low(k)
                    for grp in range(NG):
                        for q in range(grp * NOCT, (grp + 1) * NOCT):
                            o8 = (q % NOCT) * OCT
                            dve.wait_ge(s_yf, i * CV + q + 1)
                            b = buf_b[0:LINE, o8:o8 + OCT, :].rearrange("p c g -> p (c g)")
                            nc.vector.tensor_tensor(b, b, sv[0:LINE, q % 2, 1, :], ALU.mult).then_inc(s_yr, 1)
                        dve.wait_ge(s_yr, START + i * CV + (grp + 1) * NOCT)
                        per = LC // CH
                        for c in range(NLC + 2):
                            if c < NLC:
                                line_stats(grp, c)
                            if 1 <= c <= NLC:
                                lines_out(grp, c - 1)
                            if c >= 2 and grp < NG - 1:
                                for k in range((c - 2) * per, (c - 1) * per):
                                    v_low((grp + 1) * NCHK + k)
                    assert chain[0] == CHAIN


CHAIN_PER_CHUNK = 4
BU_PARTS = 5
DVE_NATURAL = BU_PARTS + 1 + TAPS + 2
DVE_EVAC = DVE_NATURAL + 7
POOL_CONSTS = 22


def experts(nc, g):
    x_v, z_rows, z_cols, out_v = g["x_v"], g["z_rows"], g["z_cols"], g["out_v"]
    ident, mean_w, mhalf, var_sel, row_sel = g["ident"], g["mean_w"], g["mhalf"], g["var_sel"], g["row_sel"]
    wout_hi, wout_lo, proj_b = g["wout_hi"], g["wout_lo"], g["proj_b"]
    bank, pair = g["psum"], g["pairs"]
    ctx = ExitStack()
    with ctx:
        def sb(name, shape, dt=F32):
            return ctx.enter_context(nc.sbuf_tensor(name, shape, dt))

        def sem(name):
            return ctx.enter_context(nc.semaphore(name))

        x1 = sb("x1", [128, N])
        zr = sb("zr", [128, N])
        zc = sb("zc", [128, W, H])
        tok_hi = sb("tok_hi", [128, N], BF16)
        tok_lo = sb("tok_lo", [128, N], BF16)
        z_hi = sb("z_hi", [128, 2, TB], BF16)
        z_lo = sb("z_lo", [128, 2, TB], BF16)
        sq = sb("sq_b", [128, 2, TB])
        hf = sb("hf_b", [128, 2, TB])
        vr = sb("vr_b", [RSTD_ROWS, 4, TB])
        vparts = sb("vparts_b", [RSTD_ROWS, TB], BF16)[:, :]
        rw_hi = sb("rw_hi", [128, E], BF16)
        rw_lo = sb("rw_lo", [128, E], BF16)
        rw = sb("rw", [128, E])
        rb_row = sb("rb_row", [1, E])
        ones_row = sb("ones_row", [1, 128])
        rb = sb("rb", [128, E])
        order = sb("order", [128, E])
        ew_hi = sb("ew_hi", [128, E, C], BF16)
        ew_lo = sb("ew_lo", [128, E, C], BF16)
        eb3 = sb("eb3", [3, E * C], BF16)
        ones3 = sb("ones3_b", [3, 128], BF16)
        lg = sb("lg", [128, TT, E])
        oh = sb("oh", [128, TT, E])
        l2 = sb("l2", [128, TT, E])
        gate = sb("gate", [128, TT, E])
        m1 = sb("m1", [128, TT])
        m2 = sb("m2", [128, TT])
        acc = sb("acc", [128, 2, C])
        part = sb("part", [128, 2, 4, C])
        fin = sb("fin", [128, 2, C])
        res = sb("res", [128, 2, TB])

        s_load = sem("expert_weights_loaded")
        s_pc = sem("expert_pool_constants")
        s_dv = sem("expert_dve_step")
        s_pe = sem("expert_pe_step")

        ew = x1[:, 0:E * C].rearrange("p (e c) -> p e c", e=E)
        eb_row = x1[0:1, 2 * E * C:3 * E * C]
        eb_res = x1[0:1, 3 * E * C:4 * E * C]
        eb_part = x1[0:1, 4 * E * C:6 * E * C].bitcast(BF16)[:, 0:3 * E * C].rearrange("p (k n) -> p k n", k=3)

        with nc.Block() as block:
            @block.sync
            def _(sp):
                sp.dma_start(ew, g["expert_w"].rearrange("e d c -> d e c")).then_inc(s_load, 16)
                sp.dma_start(rw[:, :], g["router_w"]).then_inc(s_load, 16)
                sp.dma_start(rb_row[:, :], g["router_b"].rearrange("(a e) -> a e", a=1)).then_inc(s_load, 16)
                sp.dma_start(eb_row, g["expert_b"].rearrange("(a e) c -> a (e c)", a=1)).then_inc(s_load, 16)
                sp.wait_ge(s_dv, 3 + 5)
                for k in range(3):
                    sp.dma_start(eb3[k:k + 1, :], eb_part[:, k, :]).then_inc(s_load, 16)
                sp.wait_ge(s_load, 16 * 7)

            @block.gpsimd
            def _(pool):
                nc.gpsimd.memset(ones3[:, :], 1.0).then_inc(s_pc, 1)
                nc.gpsimd.memset(ones_row[:, :], 1.0).then_inc(s_pc, 1)
                for e in range(E):
                    nc.gpsimd.memset(order[:, e:e + 1], float(E - e)).then_inc(s_pc, 1)
                pool.wait_ge(s_pc, 2 + E)

            @block.tensor
            def _(pe):
                pe.wait_ge(s_load, 16 * 4)
                pe.wait_ge(s_pc, 2 + E)
                nc.tensor.matmul(bank[0][:, 0:E], ones_row[:, :], rb_row[:, :], start=True, stop=True).then_inc(s_pe, 1)

            @block.vector
            def _(dve):
                step = [0]

                def done(ins):
                    step[0] += 1
                    ins.then_inc(s_dv, 1)
                    dve.wait_ge(s_dv, step[0])
                dve.wait_ge(s_load, 16 * 4)
                done(nc.vector.tensor_copy(ew_hi[:, :, :], ew))
                done(nc.vector.tensor_tensor(ew_lo[:, :, :], ew, ew_hi[:, :, :], ALU.subtract))
                done(nc.vector.tensor_copy(eb_part[:, 0, :], eb_row))
                done(nc.vector.tensor_tensor(eb_res, eb_row, eb_part[:, 0, :], ALU.subtract))
                done(nc.vector.tensor_copy(eb_part[:, 1, :], eb_res))
                done(nc.vector.tensor_tensor(eb_row, eb_res, eb_part[:, 1, :], ALU.subtract))
                done(nc.vector.tensor_copy(eb_part[:, 2, :], eb_row))
                done(nc.vector.tensor_copy(rw_hi[:, :], rw[:, :]))
                done(nc.vector.tensor_tensor(rw_lo[:, :], rw[:, :], rw_hi[:, :], ALU.subtract))
                dve.wait_ge(s_pe, 1)
                done(nc.vector.tensor_copy(rb[:, :], bank[0][:, 0:E]))

        s_zr = sem("z_rows_loaded")
        s_zc = sem("z_cols_loaded")
        XL = 8
        s_x = [sem(f"residual_x_loaded_{p}") for p in range(XL)]
        s_za = sem("z_summed")
        s_zh = sem("z_high_done")
        s_zl = sem("z_low_done")
        s_pj = sem("projected")
        s_x1 = sem("x1_done")
        s_mean = sem("token_mean_done")
        s_xc = sem("token_centred")
        s_sq = sem("token_squared")
        s_var = sem("token_var_done")
        s_root = sem("token_rstd_done")
        s_inv = sem("token_inverse_variance_done")
        s_sqrt = sem("token_root_done")
        s_ln = sem("token_rstd_chain")
        s_bc = sem("token_rstd_broadcast")
        s_hf = sem("token_norm_done")
        s_th = sem("token_high_done")
        s_tl = sem("token_low_done")
        s_rt = sem("logits_done")
        s_ch = sem("gate_chain")
        s_ge = sem("gate_exponent_wanted")
        s_ex = sem("gate_exponent_done")
        s_gate = sem("gates_done")
        s_ea = sem("experts_0_3_done")
        s_eb = sem("experts_4_7_done")
        s_acc = sem("experts_0_3_gated")
        s_part = sem("experts_4_7_gated")
        s_pl = sem("pool_sum_step")
        s_fin = sem("experts_summed")
        s_gs = sem("gated_sum_step")
        s_tr = sem("sum_transposed")
        s_res = sem("result_done")
        s_st = [sem(f"result_stored_{i}") for i in range(2)]

        TPB = TT // 2
        from_one = (s_x1, s_res, s_xc, s_pj, s_var, s_hf, s_tl, s_fin, s_tr, s_st[0], s_st[1])

        with nc.Block() as block:
            @block.sync
            def _(sp):
                def load_x(i, p):
                    sp.dma_start(x1[:, p * (N // XL):(p + 1) * (N // XL)],
                                 x_v[bass.ds(i, 1), :, p * (N // XL):(p + 1) * (N // XL)].rearrange("b c n -> (b c) n")
                                 ).then_inc(s_x[p], 16)

                def load_z(i):
                    sp.dma_start(zr[:, :], z_rows[bass.ds(i, 1), :, :].rearrange("b c n -> (b c) n")).then_inc(s_zr, 16)
                    sp.dma_start(zc[:, :, :].rearrange("p w h -> p (w h)"),
                                 z_cols[bass.ds(i, 1), :, :].rearrange("b c n -> (b c) n")).then_inc(s_zc, 16)

                def store(i, n):
                    sp.dma_start(out_v[bass.ds(i, 1), :, n * TB:(n + 1) * TB].rearrange("b c n -> (b c) n"),
                                 res[:, n % 2, :]).then_inc(s_st[n % 2], 16)

                load_z(0)
                for p in range(XL):
                    load_x(0, p)
                with sp.Fori(1, B) as i:
                    sp.wait_ge(s_hf, START + i * NTB)
                    load_z(i)
                    for n in range(NTB):
                        sp.wait_ge(s_res, START + i * NTB - NTB + n + 1)
                        store(i - 1, n)
                        if (n + 1) % (NTB // XL) == 0:
                            load_x(i, n // (NTB // XL))
                for n in range(NTB):
                    sp.wait_ge(s_res, START + (B - 1) * NTB + n + 1)
                    store(B - 1, n)
                for p in range(2):
                    sp.wait_ge(s_st[p], START + 16 * B * NTB // 2)

            def tb(n):
                return slice(n * TB, (n + 1) * TB)

            @block.tensor
            def _(pe):
                with pe.Fori(0, B) as i:
                    def project(n):
                        pe.wait_ge(s_zl, i * NTB + n + 1)
                        pe.wait_ge(s_x1, START + i * NTB + max(n - 1, 0))
                        if n == 0:
                            pe.wait_ge(s_res, START + i * NTB)
                        for k, (a, b) in enumerate(((wout_hi, z_hi), (wout_hi, z_lo), (wout_lo, z_hi))):
                            mm = nc.tensor.matmul(bank[n % 2][:, 0:TB], a[:, :], b[:, n % 2, :], start=(k == 0), stop=(k == 2))
                        mm.then_inc(s_pj, 1)

                    def mean(n):
                        pe.wait_ge(s_x1, START + i * NTB + n + 1)
                        pe.wait_ge(s_xc, START + i * NTB + n)
                        nc.tensor.matmul(bank[2][:, 0:TB], mean_w[:, :], x1[:, tb(n)], start=True, stop=True).then_inc(s_mean, 1)

                    def var(n):
                        pe.wait_ge(s_sq, i * NTB + n + 1)
                        nc.tensor.matmul(bank[3][0:RSTD_ROWS, 0:TB], var_sel[:, 31 - n:31 - n + RSTD_ROWS], sq[:, n % 2, :],
                                         start=(n == 0), stop=(n == NTB - 1)).then_inc(s_var, 1)

                    def spread(n):
                        if n >= 2:
                            pe.wait_ge(s_hf, START + i * NTB + n - 1)
                        else:
                            pe.wait_ge(s_root, i + 1)
                        nc.tensor.matmul(bank[n % 2][:, 0:TB], row_sel[:, n:n + 1].to_broadcast([RSTD_ROWS, 128]), vparts,
                                         start=True, stop=True).then_inc(s_bc, 1)

                    for n in range(NTB + 2):
                        if n < NTB:
                            project(n)
                        if 1 <= n <= NTB:
                            mean(n - 1)
                        if n >= 2:
                            var(n - 2)
                    for n in range(NTB):
                        spread(n)

                    pe.wait_ge(s_tl, START + (i + 1) * NTB)
                    for t in range(TT):
                        ts = slice(t * 128, (t + 1) * 128)
                        o = pair[0][:, t // TPB, (t % TPB) * E:(t % TPB + 1) * E]
                        for k, (a, b) in enumerate(((tok_hi, rw_hi), (tok_hi, rw_lo), (tok_lo, rw_hi))):
                            mm = nc.tensor.matmul(o, a[:, ts], b[:, :], start=(t % TPB == 0 and k == 0), stop=(k == 2),
                                                  skip_group_check=True)
                    mm.then_inc(s_rt, 1)

                    def expert(t):
                        ts = slice(t * 128, (t + 1) * 128)
                        for half, (free, done) in enumerate(((s_acc, s_ea), (s_part, s_eb))):
                            if t >= 2:
                                pe.wait_ge(free, i * TT + t - 1)
                            o = pair[half][:, t % 2, :]
                            es = slice(half * 4, half * 4 + 4)
                            nc.tensor.matmul(o, ones3[:, :], eb3[:, half * 4 * C:(half + 1) * 4 * C], start=True, stop=False)
                            for k, (a, b) in enumerate(((tok_hi, ew_hi), (tok_hi, ew_lo), (tok_lo, ew_hi))):
                                mm = nc.tensor.matmul(o, a[:, ts], b[:, es, :].rearrange("p e c -> p (e c)"),
                                                      start=False, stop=(k == 2))
                            mm.then_inc(done, 1)

                    def turn(t):
                        pe.wait_ge(s_fin, START + i * TT + t + 1)
                        n = t // TPC
                        if t % TPC == 0:
                            if n >= 2:
                                pe.wait_ge(s_res, START + i * NTB + n - 1)
                        mm = nc.tensor.transpose(bank[n % 2][:, (t % TPC) * 128:(t % TPC + 1) * 128], fin[:, t % 2, :],
                                                 ident[:, :])
                        mm.then_inc(s_tr, 1)

                    pe.wait_ge(s_gate, i + 1)
                    for t in range(TT + 2):
                        if t < TT:
                            expert(t)
                        if t >= 2:
                            turn(t - 2)

            @block.scalar
            def _(act):
                with act.Fori(0, B) as i:
                    def z_high(n):
                        act.wait_ge(s_za, i * NTB + n + 1)
                        act.wait_ge(s_pj, START + i * NTB + max(n - 1, 0))
                        nc.scalar.activation(z_hi[:, n % 2, :], zr[:, tb(n)], ACT.Copy).then_inc(s_zh, 1)

                    def square(n):
                        act.wait_ge(s_xc, START + i * NTB + n + 1)
                        act.wait_ge(s_var, START + i * NTB + max(n - 1, 0))
                        nc.scalar.activation(sq[:, n % 2, :], zr[:, tb(n)], ACT.Square).then_inc(s_sq, 1)

                    def high(n):
                        act.wait_ge(s_hf, START + i * NTB + n + 1)
                        nc.scalar.activation(tok_hi[:, tb(n)], hf[:, n % 2, :], ACT.Copy).then_inc(s_th, 1)

                    for n in range(NTB + 2):
                        if n < NTB:
                            z_high(n)
                        if n >= 2:
                            square(n - 2)
                    act.wait_ge(s_inv, i + 1)
                    nc.scalar.activation(vr[:, 2, :], vr[:, 1, :], ACT.Sqrt).then_inc(s_sqrt, 1)
                    for n in range(NTB):
                        high(n)

                    act.wait_ge(s_ge, i + 1)
                    nc.scalar.activation(gate[:, :, :], lg[:, :, :], ACT.Exp).then_inc(s_ex, 1)

                    act.wait_ge(s_gate, i + 1)
                    for t in range(TT):
                        act.wait_ge(s_eb, i * TT + t + 1)
                        act.wait_ge(s_fin, START + i * TT + max(t - 1, 0))
                        for e in range(4):
                            last = nc.scalar.activation(part[:, t % 2, e, :], pair[1][:, t % 2, e * C:(e + 1) * C], ACT.Copy,
                                                        scale=gate[:, t, 4 + e:5 + e])
                        last.then_inc(s_part, 1)

            @block.gpsimd
            def _(pool):
                for s in from_one:
                    pool.sem_inc(s, START)
                with pool.Fori(0, B) as i:
                    def z_low(n):
                        pool.wait_ge(s_zh, i * NTB + n + 1)
                        nc.gpsimd.tensor_tensor(z_lo[:, n % 2, :], zr[:, tb(n)], z_hi[:, n % 2, :], ALU.subtract
                                                ).then_inc(s_zl, 1)

                    def low(n):
                        pool.wait_ge(s_th, i * NTB + n + 1)
                        nc.gpsimd.tensor_tensor(tok_lo[:, tb(n)], hf[:, n % 2, :], tok_hi[:, tb(n)], ALU.subtract
                                                ).then_inc(s_tl, 1)

                    for n in range(NTB):
                        z_low(n)
                    for n in range(NTB):
                        low(n)

                    for t in range(TT):
                        pool.wait_ge(s_part, i * TT + t + 1)
                        p = part[:, t % 2, :, :]
                        nc.gpsimd.tensor_tensor(p[:, 0:2, :], p[:, 0:2, :], p[:, 2:4, :], ALU.add).then_inc(s_pl, 1)
                        pool.wait_ge(s_pl, i * (2 * TT) + 2 * t + 1)
                        nc.gpsimd.tensor_tensor(p[:, 0, :], p[:, 0, :], p[:, 1, :], ALU.add).then_inc(s_pl, 1)
                        pool.wait_ge(s_pl, i * (2 * TT) + 2 * t + 2)
                        pool.wait_ge(s_acc, i * TT + t + 1)
                        pool.wait_ge(s_tr, START + i * TT + max(t - 1, 0))
                        nc.gpsimd.tensor_tensor(fin[:, t % 2, :], p[:, 0, :], acc[:, t % 2, :], ALU.add).then_inc(s_fin, 1)

            @block.vector
            def _(dve):
                with dve.Fori(0, B) as i:
                    chain = [0]

                    def link(ins):
                        chain[0] += 1
                        ins.then_inc(s_ch, 1)
                        dve.wait_ge(s_ch, i * GATE_CHAIN + chain[0])

                    def z_sum(n):
                        if n == 0:
                            dve.wait_ge(s_zr, i * 16 + 16)
                            dve.wait_ge(s_zc, i * 16 + 16)
                        rows = TB // W
                        v = zr[:, tb(n)].rearrange("p (h w) -> p h w", w=W)
                        nc.vector.tensor_tensor(v, v, zc[:, :, n * rows:(n + 1) * rows].rearrange("p w h -> p h w"), ALU.add
                                                ).then_inc(s_za, 1)

                    def residual(n):
                        dve.wait_ge(s_x[n // (NTB // XL)], i * 16 + 16)
                        dve.wait_ge(s_pj, START + i * NTB + n + 1)
                        nc.vector.scalar_tensor_tensor(out=x1[:, tb(n)], in0=bank[n % 2][:, 0:TB], scalar=proj_b[:, :],
                                                       in1=x1[:, tb(n)], op0=ALU.add, op1=ALU.add).then_inc(s_x1, 1)

                    def centre(n):
                        dve.wait_ge(s_mean, i * NTB + n + 1)
                        nc.vector.tensor_tensor(zr[:, tb(n)], x1[:, tb(n)], bank[2][:, 0:TB], ALU.subtract
                                                ).then_inc(s_xc, 1)

                    def normal(n):
                        dve.wait_ge(s_bc, i * NTB + n + 1)
                        dve.wait_ge(s_tl, START + i * NTB + max(n - 1, 0))
                        nc.vector.tensor_tensor(hf[:, n % 2, :], zr[:, tb(n)], bank[n % 2][:, 0:TB], ALU.mult).then_inc(s_hf, 1)

                    for n in range(NTB + 2):
                        if n < NTB:
                            z_sum(n)
                        if 1 <= n <= NTB:
                            residual(n - 1)
                        if n >= 2:
                            centre(n - 2)
                    dve.wait_ge(s_var, START + (i + 1) * NTB)
                    rstd_rows(nc, dve, i, vr, vparts, bank[3][0:RSTD_ROWS, 0:TB], EPS_TOK, s_ln, s_inv, s_sqrt, s_root)
                    for n in range(NTB):
                        normal(n)

                    dve.wait_ge(s_rt, i + 1)
                    wide = [128, TT, E]
                    ob = order[:, :].unsqueeze(1).to_broadcast(wide)

                    def spread(t):
                        return t[:, :].unsqueeze(2).to_broadcast(wide)
                    for half in range(2):
                        ts = slice(half * TPB, (half + 1) * TPB)
                        last = nc.vector.tensor_tensor(lg[:, ts, :],
                                                       pair[0][:, half, 0:TPB * E].rearrange("p (t e) -> p t e", e=E),
                                                       rb[:, :].unsqueeze(1).to_broadcast([128, TPB, E]), ALU.add)
                    link(last)

                    def first_largest(src, m, dst):
                        link(nc.vector.tensor_reduce(m[:, :], src[:, :, :], AX.X, ALU.max))
                        link(nc.vector.tensor_tensor(dst[:, :, :], src[:, :, :], spread(m), ALU.is_equal))
                        link(nc.vector.tensor_tensor(dst[:, :, :], dst[:, :, :], ob, ALU.mult))
                        link(nc.vector.tensor_reduce(m2[:, :], dst[:, :, :], AX.X, ALU.max))
                        link(nc.vector.tensor_tensor(dst[:, :, :], ob, spread(m2), ALU.is_equal))

                    first_largest(lg, m1, oh)
                    link(nc.vector.scalar_tensor_tensor(out=l2[:, :, :].rearrange("p t e -> p (t e)"),
                                                        in0=oh[:, :, :].rearrange("p t e -> p (t e)"), scalar=-1e30,
                                                        in1=lg[:, :, :].rearrange("p t e -> p (t e)"),
                                                        op0=ALU.mult, op1=ALU.add))
                    nc.vector.tensor_tensor(lg[:, :, :], lg[:, :, :], spread(m1), ALU.subtract).then_inc(s_ge, 1)
                    dve.wait_ge(s_ge, i + 1)
                    first_largest(l2, m1, l2)
                    link(nc.vector.tensor_tensor(oh[:, :, :], oh[:, :, :], l2[:, :, :], ALU.add))
                    dve.wait_ge(s_ex, i + 1)
                    link(nc.vector.tensor_tensor(gate[:, :, :], gate[:, :, :], oh[:, :, :], ALU.mult))
                    link(nc.vector.tensor_reduce(m1[:, :], gate[:, :, :], AX.X, ALU.add))
                    link(nc.vector.reciprocal(m2[:, :], m1[:, :]))
                    nc.vector.tensor_tensor(gate[:, :, :], gate[:, :, :], spread(m2), ALU.mult).then_inc(s_gate, 1)
                    dve.wait_ge(s_gate, i + 1)
                    assert chain[0] == GATE_CHAIN

                    def gated(t):
                        dve.wait_ge(s_ea, i * TT + t + 1)
                        dve.wait_ge(s_fin, START + i * TT + max(t - 1, 0))
                        a = acc[:, t % 2, :]
                        nc.vector.tensor_scalar(a, pair[0][:, t % 2, 0:C], gate[:, t, 0:1], None, ALU.mult).then_inc(s_gs, 1)
                        for e in range(1, 4):
                            dve.wait_ge(s_gs, i * (3 * TT) + 3 * t + e)
                            last = nc.vector.scalar_tensor_tensor(out=a, in0=pair[0][:, t % 2, e * C:(e + 1) * C],
                                                                  scalar=gate[:, t, e:e + 1], in1=a,
                                                                  op0=ALU.mult, op1=ALU.add)
                            last.then_inc(s_gs if e < 3 else s_acc, 1)

                    def result(n):
                        dve.wait_ge(s_tr, START + i * TT + (n + 1) * TPC)
                        dve.wait_ge(s_st[n % 2], START + i * (16 * (NTB // 2)) + 16 * (n // 2))
                        nc.vector.tensor_tensor(res[:, n % 2, :], bank[n % 2][:, 0:TB], x1[:, tb(n)], ALU.add
                                                ).then_inc(s_res, 1)

                    LAG = TPC + 3
                    for t in range(TT + LAG):
                        if t < TT:
                            gated(t)
                        if t >= LAG and (t - LAG) % TPC == 0:
                            result((t - LAG) // TPC)
                    assert (TT - 1) // TPC * TPC <= TT + LAG - 1 - LAG


GATE_CHAIN = 1 + 5 + 1 + 5 + 1 + 3

_INS = ['x', 'L0_conv_W_in', 'L0_conv_b_in', 'L0_conv_dw_w', 'L0_conv_dw_b', 'L0_conv_gamma', 'L0_conv_beta',
        'L0_conv_W_out', 'L0_conv_b_out', 'L0_ffn_router_w', 'L0_ffn_router_b', 'L0_ffn_expert_w', 'L0_ffn_expert_b']


def kernel(**inputs):
    import numpy as _np
    import concourse.bacc as _bacc
    from concourse import mybir as _mybir
    from concourse.bass_utils import run_bass_kernel_spmd as _run

    nc = _bacc.Bacc("TRN2", target_bir_lowering=False, num_devices=1)
    arrays, args = {}, []
    for name in _INS:
        a = _np.ascontiguousarray(inputs[name])
        arrays[f"in_{name}"] = a
        args.append(nc.dram_tensor(f"in_{name}", a.shape, _mybir.dt.from_np(a.dtype), kind="ExternalInput").ap())
    args.append(nc.dram_tensor("out_0", (B, C, H, W), F32, kind="ExternalOutput").ap())
    build(nc, *args)
    r = _run(nc, [arrays], core_ids=[0])
    return r.results[0]["out_0"]
```

```python
import concourse.bass as bass
from concourse import mybir
from contextlib import ExitStack

F32 = mybir.dt.float32
BF16 = mybir.dt.bfloat16
F16 = mybir.dt.float16
ALU = mybir.AluOpType
ACT = mybir.ActivationFunctionType
AX = mybir.AxisListType

B, C, H, W = 8, 128, 96, 96
N = H * W
TAPS = 7
HALO = TAPS // 2
LINE = 96
WIN = LINE + 2 * HALO
KV = WIN + 1
GL = LINE // 2
NG = 4
CH = 4
NCHK = GL // CH
OCT = 8
NOCT = C // OCT
LC = 4
NLC = GL // LC
LN1 = 3 * W
NLN1 = N // LN1
RSTD_ROWS = 3 * 32
START = 1
EPS_LNC, EPS_MIX, EPS_TOK = 1e-6, 1e-5, 1e-5
H_SCALE = 16.0
W_TOP = 16.0
T_TOP = 1024.0
BV_TOP = 64.0
ONE = 4096.0
ONE_F16 = 0x6C00
Z_SCALE = 64.0
TINY = 1e-18
NHF = 3
E = 8
TB = 4 * W
NTB = N // TB
TT = N // 128
TPC = TB // 128


def build(nc, x, w_in, b_in, dw_w, dw_b, gamma, beta, w_out, b_out, router_w, router_b, expert_w, expert_b, out):
    x_v = x.rearrange("b c h w -> b c (h w)")
    out_v = out.rearrange("b c h w -> b c (h w)")
    z_rows = nc.dram_tensor("z_rows", [B, C, N], F32).ap()
    z_cols = nc.dram_tensor("z_cols", [B, C, N], F32).ap()

    top = ExitStack()
    with top:
        def keep(name, shape, dt=F32):
            return top.enter_context(nc.sbuf_tensor(name, shape, dt))

        ident = keep("ident", [128, 128])
        mean_w = keep("mean_w", [128, 128])
        mhalf = keep("mhalf", [128, 1])
        var_sel = keep("var_sel", [128, 31 + RSTD_ROWS])
        row_sel = keep("row_sel", [RSTD_ROWS, 32], BF16)
        wout_hi = keep("wout_hi", [128, 128], F16)
        wout_lo = keep("wout_lo", [128, 128], F16)
        scales = keep("scales", [128, 8])
        proj_b = keep("proj_b", [128, 1])
        psum = [top.enter_context(nc.psum_tensor(f"bank{i}", [128, 512], F32)) for i in range(4)]
        pairs = [top.enter_context(nc.psum_tensor(f"pair{i}", [128, 2, 512], F32)) for i in range(2)]

        mixer(nc, locals())
        experts(nc, locals())


def rstd_rows(nc, dve, i, vr, vparts, var, eps, s_ln, s_inv, s_sqrt, s_root):
    step = [0]

    def link(ins):
        step[0] += 1
        ins.then_inc(s_ln, 1)
        dve.wait_ge(s_ln, i * LN_CHAIN + step[0])
    link(nc.vector.tensor_scalar(vr[:, 0, :], var, eps, None, ALU.add))
    nc.vector.reciprocal(vr[:, 1, :], vr[:, 0, :]).then_inc(s_inv, 1)
    dve.wait_ge(s_sqrt, i + 1)
    link(nc.vector.tensor_tensor(vr[:, 3, :], vr[:, 2, :], vr[:, 2, :], ALU.mult))
    link(nc.vector.tensor_tensor(vr[:, 3, :], vr[:, 3, :], vr[:, 0, :], ALU.mult))
    link(nc.vector.tensor_scalar(vr[:, 3, :], vr[:, 3, :], -0.5 * H_SCALE, 1.5 * H_SCALE, ALU.mult, ALU.add))
    link(nc.vector.tensor_tensor(vr[:, 3, :], vr[:, 3, :], vr[:, 2, :], ALU.mult))
    link(nc.vector.tensor_copy(vparts, vr[:, 3, :]))
    link(nc.vector.tensor_tensor(vr[:, 0, :], vr[:, 3, :], vparts, ALU.subtract))
    nc.vector.tensor_copy(vparts[32:64, :], vr[32:64, 0, :])
    link(nc.vector.tensor_copy(vparts[64:96, :], vr[64:96, 0, :]))
    link(nc.vector.tensor_tensor(vr[64:96, 1, :], vr[64:96, 0, :], vparts[64:96, :], ALU.subtract))
    nc.vector.tensor_copy(vparts[64:96, :], vr[64:96, 1, :]).then_inc(s_root, 1)


LN_CHAIN = 9


def mixer(nc, g):
    x_v, z_rows, z_cols = g["x_v"], g["z_rows"], g["z_cols"]
    ident, mean_w, mhalf, var_sel, row_sel = g["ident"], g["mean_w"], g["mhalf"], g["var_sel"], g["row_sel"]
    wout_hi, wout_lo, proj_b, scales = g["wout_hi"], g["wout_lo"], g["proj_b"], g["scales"]
    vbank, ubank, pair = g["psum"][0:2], g["psum"][2:4], g["pairs"]
    ctx = ExitStack()
    with ctx:
        def sb(name, shape, dt=F32):
            return ctx.enter_context(nc.sbuf_tensor(name, shape, dt))

        def sem(name):
            return ctx.enter_context(nc.semaphore(name))

        TL, HL = LINE * 2 * C, (H + 2 * HALO) * W
        t_h = sb("t_h", [128, 2 * TL + HL], F16)
        t_lo = t_h[:, 0:TL].rearrange("p (m d c) -> p m d c", m=LINE, d=2)
        t_hi = t_h[:, TL:2 * TL].rearrange("p (m d c) -> p m d c", m=LINE, d=2)
        h_hi = t_h[:, 2 * TL:].rearrange("p (r w) -> p r w", w=W)
        bufs = sb("bufs", [128, 2, C, GL])
        buf_b = bufs[:, 0, :, :]
        y_f = bufs[:, 1, :, :]
        buf_a = y_f.rearrange("p c g -> p (c g)").bitcast(F16).rearrange("p (c g t) -> p c g t", c=C, t=2)
        xc = bufs[:, :, :, :].rearrange("p s c g -> p (s c g)")[:, 0:N]
        OVER = -(-(N - C * GL) // GL)
        h_lo = sb("h_lo", [128, H + 2 * HALO, W], F16)
        sq = sb("sq", [128, 2, LN1])
        hf = sb("hf", [128, NHF, LN1])
        sv = sb("sv", [128, 2, 2, OCT * GL])
        sv_flat = sv[0:RSTD_ROWS, :, :, :].rearrange("p a b n -> p (a b n)")
        vr = sv_flat[:, 0:4 * LN1].rearrange("p (k n) -> p k n", k=4)
        vparts = sb("vparts", [RSTD_ROWS, LN1], BF16)[:, :]
        zt = sb("zt", [128, 2, CH * LINE])
        win_hi = sb("win_hi", [128, 2, C], F16)
        win_lo = sb("win_lo", [128, 2, C], F16)
        stats = sb("stats", [128, LC, 2, 6])
        st = sb("st", [128, 7, LC, 2])
        rstd = sb("rstd", [128, 2, LC, 2])
        ones3 = sb("ones3", [3, 128], BF16)
        bu3 = sb("bu3", [3, CH, C], BF16)
        negbv = sb("negbv", [1, C])
        edge = sb("edge", [1, 2, 128])

        s_load = sem("weights_loaded")
        s_pc = sem("pool_constants")
        s_dv = sem("dve_step")
        s_ac = sem("act_step")
        s_pe = sem("pe_step")
        s_ready = sem("mixer_weights_ready")

        wctx = ExitStack()
        with wctx:
            def ws(name, shape, dt=F32):
                return wctx.enter_context(nc.sbuf_tensor(name, shape, dt))
            win_n = buf_b[:, 0:6, :].rearrange("p c g -> p (c g)")[:, 0:2 * C].rearrange("p (s d) -> p s d", s=2)
            wout_n = buf_b[:, 6:9, :].rearrange("p c g -> p (c g)")[:, 0:C]
            wf = buf_b[:, 9:15, :].rearrange("p c g -> p (c g)")[:, 0:2 * C].rearrange("p (s d) -> p s d", s=2)
            wof = buf_b[:, 15:18, :].rearrange("p c g -> p (c g)")[:, 0:C]
            dwn = buf_b[:, 18, 0:TAPS]
            dwr = buf_b[:, 19, 0:TAPS]
            tap_hl = buf_b[0:TAPS, 67:73, :].rearrange("p c g -> p (c g)").bitcast(F16)[:, 0:4 * C]
            cb_hl = buf_b[0:1, 73:79, :].rearrange("p c g -> p (c g)").bitcast(F16)[:, 0:4 * C]
            cols = buf_b[:, 20, 0:6]
            tmp = buf_b[:, 21, 0:2]
            taps = buf_b[0:TAPS, 22:28, :].rearrange("p c g -> p (c g)")[:, 0:2 * C]
            cb_row = buf_b[0:1, 28:34, :].rearrange("p c g -> p (c g)")[:, 0:2 * C]
            bu_row = buf_b[0:1, 34:37, :].rearrange("p c g -> p (c g)")[:, 0:C]
            bu_res = buf_b[0:1, 37:40, :].rearrange("p c g -> p (c g)")[:, 0:C]
            zband = buf_b[0:TAPS, 40:46, :].rearrange("p c g -> p (c g)").bitcast(F16)[:, 0:LINE - 1 + KV]
            last = buf_b[0:1, 46:49, :].rearrange("p c g -> p (c g)").bitcast(F16)[:, 0:KV]
            bu_part = buf_b[0:1, 49:58, :].rearrange("p c g -> p (c g)").bitcast(BF16)[:, 0:3 * C]\
                .rearrange("p (k c) -> p k c", k=3)
            bv_row = buf_b[0:1, 58:61, :].rearrange("p c g -> p (c g)")[:, 0:C]
            mxs = buf_b[:, 61, 0:16]
            q = buf_b[0:1, 62, 0:8]
            srow = buf_b[0:1, 63, 0:8]
            ones_f = buf_b[0:1, 64:67, :].rearrange("p c g -> p (c g)")[:, 0:128]

            SLOTS = 4

            def slot(m):
                return pair[m % 2][0:KV, m // 2 % 2, :]

            def both_parts(m):
                return t_h[0:KV, 0:2 * TL].rearrange("p (k m n) -> p k m n", k=2, m=LINE)[:, :, m, :]

            with nc.Block() as block:
                @block.sync
                def _(sp):
                    sp.dma_start(win_n[:, :, :], g["w_in"].rearrange("(s o) d -> o s d", s=2)).then_inc(s_load, 16)
                    sp.dma_start(wout_n, g["w_out"]).then_inc(s_load, 16)
                    sp.dma_start(dwn, g["dw_w"].rearrange("c a k -> c (a k)")).then_inc(s_load, 16)
                    sp.dma_start(cols[:, 0:1], g["b_in"].rearrange("(s c a) -> s c a", s=2, a=1)[1]).then_inc(s_load, 16)
                    for n, v in enumerate(("dw_b", "gamma", "beta", "b_out")):
                        sp.dma_start(cols[:, n + 1:n + 2], g[v].rearrange("(c a) -> c a", a=1)).then_inc(s_load, 16)
                    sp.dma_start(bu_row, g["b_in"].rearrange("(s c) -> s c", s=2)[0:1]).then_inc(s_load, 16)
                    sp.dma_start(bv_row, g["b_in"].rearrange("(s c) -> s c", s=2)[1:2]).then_inc(s_load, 16)
                    sp.wait_ge(s_dv, BU_PARTS)
                    for k in range(3):
                        for j in range(CH):
                            sp.dma_start(bu3[k:k + 1, j, :], bu_part[:, k, :]).then_inc(s_load, 16)
                    sp.wait_ge(s_load, 16 * (10 + 3 * CH))

                @block.gpsimd
                def _(pool):
                    step = [0]

                    def done(ins):
                        step[0] += 1
                        ins.then_inc(s_pc, 1)
                        pool.wait_ge(s_pc, step[0])
                    done(nc.gpsimd.memset(ident[:, :], 0.0))
                    done(nc.gpsimd.affine_select(out=ident[:, :], in_=ident[:, :], compare_op=ALU.not_equal, fill=1.0,
                                                 base=0, pattern=[[-1, 128]], channel_multiplier=1))
                    done(nc.gpsimd.memset(mean_w[:, :], 1.0 / C))
                    done(nc.gpsimd.memset(mhalf[:, :], -0.5))
                    done(nc.gpsimd.memset(var_sel[:, :], 0.0))
                    done(nc.gpsimd.memset(var_sel[:, 31:31 + RSTD_ROWS:32], 1.0 / C))
                    done(nc.gpsimd.memset(row_sel[:, :], 0.0))
                    for k in range(3):
                        done(nc.gpsimd.affine_select(out=row_sel[:, :], in_=row_sel[:, :], compare_op=ALU.not_equal, fill=1.0,
                                                     base=-32 * k, pattern=[[-1, 32]], channel_multiplier=1))
                    done(nc.gpsimd.memset(zband, 0.0))
                    done(nc.gpsimd.affine_select(out=zband, in_=zband, compare_op=ALU.not_equal, fill=1.0,
                                                 base=LINE - 1, pattern=[[-1, LINE - 1 + KV]], channel_multiplier=1))
                    done(nc.gpsimd.memset(last, 0.0))
                    done(nc.gpsimd.memset(last[:, WIN:KV], 1.0))
                    done(nc.gpsimd.memset(ones3[:, :], 1.0))
                    done(nc.gpsimd.memset(ones_f, 1.0))
                    done(nc.gpsimd.memset(edge[:, :, :], 0.0))
                    done(nc.gpsimd.memset(edge[:, 0, 0:HALO], 1.0))
                    done(nc.gpsimd.memset(edge[:, 1, WIN - HALO:WIN], 1.0))
                    assert step[0] == POOL_CONSTS
                    done(nc.gpsimd.memset(h_hi[:, :, :], 0.0))
                    done(nc.gpsimd.memset(h_lo[:, :, :], 0.0))
                    done(nc.gpsimd.memset(buf_a[:, :, :, 0], ONE))
                    done(nc.gpsimd.memset(buf_a[:, :, :, 1], 0.0))

                @block.vector
                def _(dve):
                    step = [0]

                    def done(ins):
                        step[0] += 1
                        ins.then_inc(s_dv, 1)
                        dve.wait_ge(s_dv, step[0])
                    dve.wait_ge(s_load, 16 * 10)
                    done(nc.vector.tensor_scalar(wf[:, :, :], win_n[:, :, :], -1.0, None, ALU.mult))
                    done(nc.vector.tensor_reduce(mxs[:, 0:1], win_n[:, :, :].rearrange("p s d -> p (s d)"), AX.X, ALU.max))
                    done(nc.vector.tensor_reduce(mxs[:, 1:2], wf[:, :, :].rearrange("p s d -> p (s d)"), AX.X, ALU.max))
                    done(nc.vector.tensor_scalar(mxs[:, 2:3], cols[:, 0:1], 1.0 / BV_TOP, None, ALU.mult))
                    done(nc.vector.tensor_scalar(mxs[:, 3:4], cols[:, 0:1], -1.0 / BV_TOP, None, ALU.mult))
                    for j in range(TAPS):
                        done(nc.vector.tensor_copy(dwr[:, j:j + 1], dwn[:, TAPS - 1 - j:TAPS - j]))
                    done(nc.vector.reduce_sum(tmp[:, 0:1], dwn, AX.X))
                    done(nc.vector.tensor_scalar(tmp[:, 1:2], tmp[:, 0:1], cols[:, 0:1], cols[:, 1:2], ALU.mult, ALU.add))
                    done(nc.vector.tensor_reduce(mxs[:, 4:5], dwn, AX.X, ALU.max))
                    done(nc.vector.tensor_scalar(mxs[:, 8:8 + TAPS], dwn, -1.0, None, ALU.mult))
                    done(nc.vector.tensor_reduce(mxs[:, 5:6], mxs[:, 8:8 + TAPS], AX.X, ALU.max))
                    done(nc.vector.tensor_copy(mxs[:, 6:7], tmp[:, 1:2]))
                    done(nc.vector.tensor_scalar(mxs[:, 7:8], tmp[:, 1:2], -1.0, None, ALU.mult))
                    assert step[0] == DVE_NATURAL
                    dve.wait_ge(s_pe, 1)
                    done(nc.vector.tensor_copy(wf[:, :, :], vbank[0][:, 0:2 * C].rearrange("p (s d) -> p s d", s=2)))
                    done(nc.vector.tensor_copy(wof, vbank[1][:, 0:C]))
                    done(nc.vector.tensor_copy(taps, ubank[0][0:TAPS, 0:2 * C]))
                    done(nc.vector.tensor_copy(cb_row[:, 0:C], ubank[1][0:1, 0:C]))
                    done(nc.vector.tensor_copy(cb_row[:, C:2 * C], ubank[1][0:1, 0:C]))
                    done(nc.vector.tensor_reduce(q[:, 0:1], pair[0][0:1, 1, :], AX.X, ALU.max))
                    done(nc.vector.tensor_reduce(q[:, 2:3], pair[1][0:1, 1, 0:2 * C], AX.X, ALU.max))
                    done(nc.vector.tensor_reduce(q[:, 3:4], pair[1][0:1, 1, 2 * C:4 * C], AX.X, ALU.max))
                    done(nc.vector.tensor_scalar(q[:, 0:1], q[:, 0:1], TINY, None, ALU.add))
                    done(nc.vector.reciprocal(q[:, 1:2], q[:, 0:1]))
                    done(nc.vector.tensor_scalar(q[:, 3:4], q[:, 3:4], q[:, 1:2], V_SCALE / ONE, ALU.mult, ALU.mult))
                    done(nc.vector.tensor_reduce(q[:, 4:5], q[:, 2:4], AX.X, ALU.max))
                    done(nc.vector.tensor_scalar(q[:, 4:5], q[:, 4:5], TINY, None, ALU.add))
                    done(nc.vector.reciprocal(q[:, 5:6], q[:, 4:5]))
                    done(nc.vector.tensor_scalar(srow[:, 0:1], q[:, 1:2], W_TOP, None, ALU.mult))
                    done(nc.vector.tensor_scalar(srow[:, 1:2], q[:, 1:2], V_SCALE, None, ALU.mult))
                    done(nc.vector.tensor_scalar(srow[:, 2:3], q[:, 0:1], 1.0 / V_SCALE, None, ALU.mult))
                    done(nc.vector.tensor_scalar(srow[:, 3:4], q[:, 5:6], T_TOP, None, ALU.mult))
                    done(nc.vector.tensor_scalar(srow[:, 4:5], q[:, 5:6], q[:, 1:2], T_TOP * V_SCALE / ONE, ALU.mult, ALU.mult))
                    done(nc.vector.tensor_scalar(srow[:, 5:6], q[:, 4:5], q[:, 0:1], 1.0 / (T_TOP * V_SCALE), ALU.mult, ALU.mult))
                    assert step[0] == DVE_EVAC
                    dve.wait_ge(s_pe, 2)
                    done(nc.vector.tensor_copy(scales[:, 0:6], pair[0][:, 1, 0:6]))
                    done(nc.vector.tensor_tensor(proj_b[:, :], vbank[0][:, 0:1], cols[:, 4:5], ALU.add))
                    done(nc.vector.tensor_scalar(wof, wof, cols[:, 2:3], 0.25, ALU.mult, ALU.mult))
                    assert step[0] == DVE_GAMMA
                    done(nc.vector.tensor_scalar(bu_row, bu_row, scales[0:1, 1:2], None, ALU.mult))
                    done(nc.vector.tensor_copy(bu_part[:, 0, :], bu_row))
                    done(nc.vector.tensor_tensor(bu_res, bu_row, bu_part[:, 0, :], ALU.subtract))
                    done(nc.vector.tensor_copy(bu_part[:, 1, :], bu_res))
                    done(nc.vector.tensor_tensor(bu_row, bu_res, bu_part[:, 1, :], ALU.subtract))
                    done(nc.vector.tensor_copy(bu_part[:, 2, :], bu_row))
                    assert step[0] == BU_PARTS
                    done(nc.vector.tensor_scalar(negbv[:, :], bv_row, scales[0:1, 1:2], -1.0, ALU.mult, ALU.mult))
                    wf2 = wf[:, :, :].rearrange("p s d -> p (s d)")
                    done(nc.vector.tensor_scalar(wf2, wf2, scales[:, 0:1], None, ALU.mult))
                    done(nc.vector.tensor_copy(win_hi[:, :, :], wf[:, :, :]))
                    done(nc.vector.tensor_tensor(win_lo[:, :, :], wf[:, :, :], win_hi[:, :, :], ALU.subtract))
                    done(nc.vector.tensor_scalar(taps, taps, scales[0:TAPS, 3:4], None, ALU.mult))
                    done(nc.vector.tensor_scalar(cb_row, cb_row, scales[0:1, 4:5], None, ALU.mult))
                    for d in range(2):
                        lo, hi = slice(d * C, (d + 1) * C), slice((2 + d) * C, (3 + d) * C)
                        done(nc.vector.tensor_copy(tap_hl[:, hi], taps[:, lo]))
                        done(nc.vector.tensor_tensor(tap_hl[:, lo], taps[:, lo], tap_hl[:, hi], ALU.subtract))
                        done(nc.vector.tensor_copy(cb_hl[:, hi], cb_row[:, lo]))
                        done(nc.vector.tensor_tensor(cb_hl[:, lo], cb_row[:, lo], cb_hl[:, hi], ALU.subtract))
                    dve.wait_ge(s_pe, 3)
                    done(nc.vector.tensor_tensor(wof, wof, vbank[1][:, 0:C], ALU.subtract))
                    done(nc.vector.tensor_scalar(win_n[:, 0, :], wof, -1.0, None, ALU.mult))
                    done(nc.vector.tensor_reduce(mxs[:, 0:1], wof, AX.X, ALU.max))
                    done(nc.vector.tensor_reduce(mxs[:, 1:2], win_n[:, 0, :], AX.X, ALU.max))
                    assert step[0] == DVE_CENTRED
                    dve.wait_ge(s_pe, 4)
                    done(nc.vector.tensor_reduce(q[:, 6:7], pair[1][0:1, 1, 0:2 * C], AX.X, ALU.max))
                    done(nc.vector.tensor_scalar(q[:, 6:7], q[:, 6:7], TINY, None, ALU.add))
                    done(nc.vector.reciprocal(q[:, 7:8], q[:, 6:7]))
                    done(nc.vector.tensor_scalar(srow[:, 6:7], q[:, 7:8], T_TOP, None, ALU.mult))
                    done(nc.vector.tensor_scalar(srow[:, 7:8], q[:, 6:7], 1.0 / (T_TOP * Z_SCALE), None, ALU.mult))
                    assert step[0] == DVE_OUT
                    dve.wait_ge(s_pe, 5)
                    done(nc.vector.tensor_copy(scales[:, 6:8], pair[0][:, 1, 0:2]))
                    done(nc.vector.tensor_scalar(wof, wof, scales[:, 6:7], None, ALU.mult))
                    done(nc.vector.tensor_copy(wout_hi[:, :], wof))
                    done(nc.vector.tensor_tensor(wout_lo[:, :], wof, wout_hi[:, :], ALU.subtract))
                    assert step[0] == DVE_SETUP
                    for m in range(1, LINE, 2):
                        dve.wait_ge(s_pe, 6 + m)
                        nc.vector.tensor_copy(both_parts(m), slot(m).rearrange("p (k n) -> p k n", k=2)).then_inc(s_ready, 1)
                    dve.wait_ge(s_ready, LINE // 2)

                @block.scalar
                def _(act):
                    for m in range(0, LINE, 2):
                        act.wait_ge(s_pe, 6 + m)
                        nc.scalar.activation(both_parts(m), slot(m).rearrange("p (k n) -> p k n", k=2), ACT.Copy
                                             ).then_inc(s_ac, 1)
                    act.wait_ge(s_ac, LINE // 2)

                @block.tensor
                def _(pe):
                    pe.wait_ge(s_load, 16 * 10)
                    pe.wait_ge(s_pc, POOL_CONSTS)
                    pe.wait_ge(s_dv, DVE_NATURAL)
                    for n, s in enumerate((1, 0)):
                        nc.tensor.matmul(vbank[0][:, n * C:(n + 1) * C], win_n[:, s, :], ident[:, :], start=True, stop=True)
                    nc.tensor.matmul(vbank[1][:, 0:C], wout_n, ident[:, :], start=True, stop=True)
                    nc.tensor.matmul(ubank[0][0:TAPS, 0:C], dwn, ident[:, :], start=True, stop=True)
                    nc.tensor.matmul(ubank[0][0:TAPS, C:2 * C], dwr, ident[:, :], start=True, stop=True)
                    for n in range(8):
                        nc.tensor.matmul(pair[n // 4][0:1, 1, n % 4 * C:(n % 4 + 1) * C], mxs[:, n:n + 1], ident[:, :],
                                         start=True, stop=True)
                    nc.tensor.matmul(ubank[1][0:1, 0:C], tmp[:, 1:2], ident[:, :], start=True, stop=True).then_inc(s_pe, 1)
                    pe.wait_ge(s_dv, DVE_EVAC)
                    nc.tensor.matmul(pair[0][:, 1, 0:6], ones_f, srow[:, 0:6], start=True, stop=True)
                    nc.tensor.matmul(vbank[0][:, 0:1], wof, cols[:, 3:4], start=True, stop=True).then_inc(s_pe, 1)
                    pe.wait_ge(s_dv, DVE_GAMMA)
                    nc.tensor.matmul(vbank[1][:, 0:C], mean_w[:, :], wof, start=True, stop=True).then_inc(s_pe, 1)
                    pe.wait_ge(s_dv, DVE_CENTRED)
                    nc.tensor.matmul(pair[1][0:1, 1, 0:C], mxs[:, 0:1], ident[:, :], start=True, stop=True)
                    nc.tensor.matmul(pair[1][0:1, 1, C:2 * C], mxs[:, 1:2], ident[:, :], start=True, stop=True
                                     ).then_inc(s_pe, 1)
                    pe.wait_ge(s_dv, DVE_OUT)
                    nc.tensor.matmul(pair[0][:, 1, 0:2], ones_f, srow[:, 6:8], start=True, stop=True).then_inc(s_pe, 1)
                    pe.wait_ge(s_dv, DVE_SETUP)
                    for m in range(LINE):
                        if m >= SLOTS:
                            pe.wait_ge(s_ready if m % 2 else s_ac, (m - SLOTS) // 2 + 1)
                        nc.tensor.matmul(slot(m), zband[:, LINE - 1 - m:LINE - 1 - m + KV], tap_hl, start=True, stop=False)
                        nc.tensor.matmul(slot(m), last, cb_hl, start=False, stop=True).then_inc(s_pe, 1)

        XL = 8
        s_x = [sem(f"x_part_loaded_{n}") for n in range(XL)]
        s_mean = sem("mean_done")
        s_xc = sem("x_centred")
        s_sq = sem("x_squared")
        s_var = sem("var_done")
        s_root = sem("image_rstd_done")
        s_inv = sem("inverse_variance_done")
        s_sqrt = sem("root_done")
        s_ln = sem("rstd_chain")
        s_bc = sem("rstd_broadcast")
        s_one = sem("bias_row_restored")
        s_hf = sem("h_done")
        s_hh = sem("h_high_done")
        s_hl = sem("h_low_done")
        s_halo = sem("halo_rows_done")
        s_v = sem("v_product_done")
        s_u = sem("u_product_done")
        s_vh = sem("v_high_done")
        s_vl = sem("v_low_done")
        s_su = sem("silu_u_done")
        s_conv = sem("conv_done")
        s_sv = sem("silu_conv_done")
        s_yf = sem("y_forward_done")
        s_yr = sem("y_reversed_done")
        s_ch = sem("dve_chain")
        s_mv = sem("variances_ready")
        s_r = sem("line_rstd_ready")
        s_sc = sem("y_forward_scaled")
        s_sb = sem("y_reversed_scaled")
        s_z = sem("z_lines_done")
        s_tr = sem("z_transposed")
        s_zt = sem("z_copied")
        s_zst = [sem(f"z_stored_{i}") for i in range(2)]

        from_one = (s_xc, s_vl, s_su, s_zt, s_var, s_yr, s_zst[0], s_zst[1], s_hl)
        UV = NG * NCHK
        CV = NG * NOCT

        with nc.Block() as block:
            @block.sync
            def _(sp):
                with sp.Fori(0, B) as i:
                    sp.wait_ge(s_zt, START + i * UV)
                    for n in range(XL):
                        sp.dma_start(xc[:, n * (N // XL):(n + 1) * (N // XL)],
                                     x_v[bass.ds(i, 1), :, n * (N // XL):(n + 1) * (N // XL)].rearrange("b c n -> (b c) n")
                                     ).then_inc(s_x[n], 16)
                    for k in range(UV):
                        sp.wait_ge(s_zt, START + i * UV + k + 1)
                        dst = z_rows if k < UV // 2 else z_cols
                        kk = k % (UV // 2)
                        sp.dma_start(dst[bass.ds(i, 1), :, kk * CH * LINE:(kk + 1) * CH * LINE].rearrange("b c n -> (b c) n"),
                                     zt[:, k % 2, :]).then_inc(s_zst[k % 2], 16)
                for p in range(2):
                    sp.wait_ge(s_zst[p], START + 16 * B * UV // 2)

            @block.tensor
            def _(pe):
                with pe.Fori(0, B) as i:
                    def mean(n):
                        pe.wait_ge(s_x[n * XL // NLN1], i * 16 + 16)
                        if n >= 2:
                            pe.wait_ge(s_xc, START + i * NLN1 + n - 1)
                        else:
                            pe.wait_ge(s_vl, START + i * UV)
                        nc.tensor.matmul(vbank[n % 2][:, 0:LN1], mean_w[:, :], xc[:, n * LN1:(n + 1) * LN1], start=True, stop=True
                                         ).then_inc(s_mean, 1)

                    def var(n):
                        pe.wait_ge(s_sq, i * NLN1 + n + 1)
                        if n == 0:
                            pe.wait_ge(s_su, START + i * UV)
                        nc.tensor.matmul(ubank[0][0:RSTD_ROWS, 0:LN1], var_sel[:, 31 - n:31 - n + RSTD_ROWS], sq[:, n % 2, :],
                                         start=(n == 0), stop=(n == NLN1 - 1)).then_inc(s_var, 1)

                    def spread(n):
                        if n >= 2:
                            pe.wait_ge(s_hf, i * NLN1 + n - 1)
                        else:
                            pe.wait_ge(s_root, i + 1)
                        nc.tensor.matmul(vbank[n % 2][:, 0:LN1], row_sel[:, n:n + 1].to_broadcast([RSTD_ROWS, 128]), vparts,
                                         start=True, stop=True).then_inc(s_bc, 1)

                    for n in range(NLN1):
                        mean(n)
                        if n >= 1:
                            var(n - 1)
                    var(NLN1 - 1)
                    for n in range(NLN1):
                        spread(n)

                    def window(h, line, cols, lo, cnt):
                        if cols:
                            return h[:, lo:lo + cnt, line]
                        flat = h[:, :, :].rearrange("p r w -> p (r w)")
                        at = (line + HALO) * W - HALO + lo
                        return flat[:, at:at + cnt]

                    def uv(k):
                        grp, ch = divmod(k, NCHK)
                        cols = grp >= 2
                        l0 = (grp % 2) * GL + ch * CH
                        vb, ub = vbank[k % 2], ubank[k % 2]
                        if k >= 2:
                            pe.wait_ge(s_vl, START + i * UV + k - 1)
                            pe.wait_ge(s_su, START + i * UV + k - 1)
                        else:
                            pe.wait_ge(s_hf, (i + 1) * NLN1)
                        nc.tensor.matmul(ub[0:LINE, :], ones3[:, 0:LINE], bu3[:, :, :].rearrange("p j c -> p (j c)"),
                                         start=True, stop=False, skip_group_check=True)
                        for j in range(CH):
                            o = ub[0:LINE, j * C:(j + 1) * C]
                            for n, (hh, ww) in enumerate(((h_hi, win_hi), (h_hi, win_lo), (h_lo, win_hi))):
                                mm = nc.tensor.matmul(o, window(hh, l0 + j, cols, HALO, LINE), ww[:, 1, :],
                                                      start=False, stop=(n == 2), skip_group_check=True)
                        mm.then_inc(s_u, 1)
                        for j in range(CH):
                            o = vb[0:WIN, j * C:(j + 1) * C]
                            at_edge = (l0 + j) in (0, LINE - 1)
                            first = [j == 0]
                            if at_edge:
                                s = 0 if l0 + j == 0 else 1
                                nc.tensor.matmul(o, edge[:, s, 0:WIN], negbv[:, :], start=first[0], stop=False,
                                                 skip_group_check=True)
                                first[0] = False
                            for n, (hh, ww) in enumerate(((h_hi, win_hi), (h_hi, win_lo), (h_lo, win_hi))):
                                mm = nc.tensor.matmul(o, window(hh, l0 + j, cols, 0, WIN), ww[:, 0, :],
                                                      start=first[0], stop=(n == 2), skip_group_check=True)
                                first[0] = False
                        mm.then_inc(s_v, 1)

                    def conv(q):
                        o8 = (q % NOCT) * OCT
                        if q % NOCT == 0:
                            pe.wait_ge(s_vl, START + i * UV + (q // NOCT + 1) * NCHK)
                            pe.wait_ge(s_zt, START + i * UV + q // NOCT * NCHK)
                        if q % NOCT >= 2:
                            pe.wait_ge(s_sv, i * CV + q - 1)
                        for d in range(2):
                            for c in range(OCT):
                                o = pair[q % 2][:, d, c * GL:(c + 1) * GL]
                                ops = ((TL, 0), (0, 0), (TL, 1))
                                for n, (at, part) in enumerate(ops):
                                    at += d * C + o8 + c
                                    mm = nc.tensor.matmul(o, t_h[0:KV, at:at + 127 * 2 * C + 1:2 * C],
                                                          buf_a[0:KV, o8 + c, :, part],
                                                          start=(c == 0 and n == 0), stop=(n == 2), skip_group_check=True)
                        mm.then_inc(s_conv, 1)

                    def turn(k):
                        grp, ch = divmod(k, NCHK)
                        pe.wait_ge(s_z, i * NG * NLC + grp * NLC + ch * CH // LC + 1)
                        if ch >= 2:
                            pe.wait_ge(s_zt, START + i * UV + k - 1)
                        else:
                            pe.wait_ge(s_sv, i * CV + (grp + 1) * NOCT)
                        for j in range(CH):
                            mm = nc.tensor.transpose(pair[k % 2][:, 0, j * LINE:(j + 1) * LINE],
                                                     y_f[0:LINE, :, ch * CH + j], ident[0:LINE, 0:LINE])
                        mm.then_inc(s_tr, 1)

                    pe.wait_ge(s_hl, START + (i + 1) * NLN1)
                    for k in range(NCHK):
                        uv(k)
                    for grp in range(NG):
                        if grp == 1:
                            pe.wait_ge(s_halo, (i + 1) * 4)
                        for q in range(grp * NOCT, (grp + 1) * NOCT):
                            conv(q)
                        for k in range(grp * NCHK, (grp + 1) * NCHK):
                            turn(k)
                            if grp < NG - 1:
                                uv(k + NCHK)

            @block.scalar
            def _(act):
                with act.Fori(0, B) as i:
                    def square(n):
                        act.wait_ge(s_xc, START + i * NLN1 + n + 1)
                        act.wait_ge(s_var, START + i * NLN1 + max(n - 1, 0))
                        nc.scalar.activation(sq[:, n % 2, :], xc[:, n * LN1:(n + 1) * LN1], ACT.Square).then_inc(s_sq, 1)

                    def high(n):
                        act.wait_ge(s_hf, i * NLN1 + n + 1)
                        r0 = HALO + n * (LN1 // W)
                        nc.scalar.activation(h_hi[:, r0:r0 + LN1 // W, :].rearrange("p r w -> p (r w)"), hf[:, n % NHF, :],
                                             ACT.Copy).then_inc(s_hh, 1)

                    for n in range(NLN1):
                        square(n)
                    act.wait_ge(s_inv, i + 1)
                    nc.scalar.activation(vr[:, 2, :], vr[:, 1, :], ACT.Sqrt).then_inc(s_sqrt, 1)
                    for n in range(NLN1):
                        high(n)

                    def uv_out(k):
                        grp, ch = divmod(k, NCHK)
                        ls = slice(ch * CH, (ch + 1) * CH)
                        act.wait_ge(s_u, i * UV + k + 1)
                        nc.scalar.activation(buf_b[0:LINE, :, ls].rearrange("p c g -> p g c"),
                                             ubank[k % 2][0:LINE, :].rearrange("p (g c) -> p g c", g=CH), ACT.Silu,
                                             scale=scales[0:LINE, 2:3]).then_inc(s_su, 1)
                        act.wait_ge(s_v, i * UV + k + 1)
                        if k == 0:
                            act.wait_ge(s_one, i + 1)
                        nc.scalar.activation(buf_a[0:WIN, :, ls, 0].rearrange("p c g -> p g c"),
                                             vbank[k % 2][0:WIN, :].rearrange("p (g c) -> p g c", g=CH), ACT.Copy
                                             ).then_inc(s_vh, 1)

                    for k in range(NCHK):
                        uv_out(k)
                    for grp in range(NG):
                        for q in range(grp * NOCT, (grp + 1) * NOCT):
                            act.wait_ge(s_conv, i * CV + q + 1)
                            act.wait_ge(s_yr, START + i * CV + max(q - 1, 0))
                            nc.scalar.activation(sv[0:LINE, q % 2, :, :], pair[q % 2][0:LINE, :, 0:OCT * GL], ACT.Silu,
                                                 scale=scales[0:LINE, 5:6]).then_inc(s_sv, 1)
                        def scale_reversed(c):
                            act.wait_ge(s_r, i * NG * NLC + grp * NLC + c + 1)
                            for l in range(LC):
                                y = buf_b[0:LINE, :, c * LC + l]
                                last = nc.scalar.activation(y, y, ACT.Copy, scale=rstd[0:LINE, c % 2, l, 1:2])
                            last.then_inc(s_sb, 1)

                        scale_reversed(0)
                        for k in range(grp * NCHK, (grp + 1) * NCHK):
                            if k % NCHK + 1 < NLC:
                                scale_reversed(k % NCHK + 1)
                            act.wait_ge(s_tr, i * UV + k + 1)
                            act.wait_ge(s_zst[k % 2], START + i * (16 * (UV // 2)) + 16 * (k // 2))
                            nc.scalar.activation(zt[:, k % 2, :], pair[k % 2][:, 0, 0:CH * LINE], ACT.Copy).then_inc(s_zt, 1)
                            if grp < NG - 1:
                                uv_out(k + NCHK)
                        if grp == 0:
                            for h in (h_hi, h_lo):
                                nc.scalar.activation(h[:, 0:HALO, 1:W], h[:, H:H + HALO, 0:W - 1], ACT.Copy).then_inc(s_halo, 1)
                                nc.scalar.activation(h[:, H + HALO:H + 2 * HALO, 0:W - 1], h[:, HALO:2 * HALO, 1:W],
                                                     ACT.Copy).then_inc(s_halo, 1)

            @block.gpsimd
            def _(pool):
                for s in from_one:
                    pool.sem_inc(s, START)
                with pool.Fori(0, B) as i:
                    def low(n):
                        pool.wait_ge(s_hh, i * NLN1 + n + 1)
                        r0 = HALO + n * (LN1 // W)
                        o = (slice(None), slice(r0, r0 + LN1 // W), slice(None))
                        nc.gpsimd.tensor_tensor(h_lo[o].rearrange("p r w -> p (r w)"), hf[:, n % NHF, :],
                                                h_hi[o].rearrange("p r w -> p (r w)"), ALU.subtract).then_inc(s_hl, 1)

                    for h in (h_hi, h_lo):
                        nc.gpsimd.memset(h[:, HALO - 1, W - HALO:W], 0.0)
                        nc.gpsimd.memset(h[:, H + HALO, 0:HALO], 0.0)
                    for n in range(NLN1):
                        low(n)

                    for grp in range(NG):
                        for q in range(grp * NOCT, (grp + 1) * NOCT):
                            o8 = (q % NOCT) * OCT
                            pool.wait_ge(s_sv, i * CV + q + 1)
                            nc.gpsimd.tensor_tensor(y_f[0:LINE, o8:o8 + OCT, :].rearrange("p c g -> p (c g)"),
                                                    buf_b[0:LINE, o8:o8 + OCT, :].rearrange("p c g -> p (c g)"),
                                                    sv[0:LINE, q % 2, 0, :], ALU.mult).then_inc(s_yf, 1)
                        for c in range(NLC):
                            pool.wait_ge(s_mv, i * NG * NLC + grp * NLC + c + 1)
                            nc.gpsimd.tensor_tensor(rstd[0:LINE, c % 2, :, :], st[0:LINE, 5 + c % 2, :, :],
                                                    mhalf[0:LINE, 0:1].unsqueeze(2).to_broadcast([LINE, LC, 2]), ALU.pow
                                                    ).then_inc(s_r, 1)
                            pool.wait_ge(s_r, i * NG * NLC + grp * NLC + c + 1)
                            y = y_f[0:LINE, :, c * LC:(c + 1) * LC]
                            nc.gpsimd.tensor_tensor(y, y, rstd[0:LINE, c % 2, :, 0].unsqueeze(1).to_broadcast([LINE, C, LC]),
                                                    ALU.mult).then_inc(s_sc, 1)

            @block.vector
            def _(dve):
                with dve.Fori(0, B) as i:
                    CHAIN = NG * NLC * CHAIN_PER_CHUNK
                    chain = [0]

                    def link(ins):
                        chain[0] += 1
                        ins.then_inc(s_ch, 1)
                        dve.wait_ge(s_ch, i * CHAIN + chain[0])

                    def centre(n):
                        dve.wait_ge(s_mean, i * NLN1 + n + 1)
                        v = xc[:, n * LN1:(n + 1) * LN1]
                        nc.vector.tensor_tensor(v, v, vbank[n % 2][:, 0:LN1], ALU.subtract).then_inc(s_xc, 1)

                    def normal(n):
                        dve.wait_ge(s_bc, i * NLN1 + n + 1)
                        dve.wait_ge(s_hl, START + i * NLN1 + max(n - NHF + 1, 0))
                        nc.vector.tensor_tensor(hf[:, n % NHF, :], xc[:, n * LN1:(n + 1) * LN1], vbank[n % 2][:, 0:LN1],
                                                ALU.mult).then_inc(s_hf, 1)

                    for n in range(NLN1):
                        centre(n)
                    dve.wait_ge(s_var, START + (i + 1) * NLN1)
                    rstd_rows(nc, dve, i, vr, vparts, ubank[0][0:RSTD_ROWS, 0:LN1], EPS_LNC, s_ln, s_inv, s_sqrt, s_root)
                    for n in range(NLN1):
                        normal(n)
                    dve.wait_ge(s_hf, (i + 1) * NLN1)
                    nc.vector.memset(y_f[96:128, 0:OVER, :].rearrange("p c g -> p (c g)").bitcast(mybir.dt.uint32), ONE_F16
                                     ).then_inc(s_one, 1)

                    def v_low(k):
                        grp, ch = divmod(k, NCHK)
                        ls = slice(ch * CH, (ch + 1) * CH)
                        dve.wait_ge(s_vh, i * UV + k + 1)
                        nc.vector.tensor_tensor(buf_a[0:WIN, :, ls, 1].rearrange("p c g -> p g c"),
                                                vbank[k % 2][0:WIN, :].rearrange("p (g c) -> p g c", g=CH),
                                                buf_a[0:WIN, :, ls, 0].rearrange("p c g -> p g c"), ALU.subtract
                                                ).then_inc(s_vl, 1)

                    def line_stats(grp, c):
                        for l in range(LC):
                            for d, y in enumerate((y_f, buf_b)):
                                ins = nc.vector.bn_stats(stats[0:LINE, l, d, :], y[0:LINE, :, c * LC + l])
                        link(ins)
                        s = [stats[0:LINE, :, :, n] for n in range(6)]
                        nc.vector.tensor_tensor(st[0:LINE, 0, :, :], s[1], s[4], ALU.subtract)
                        link(nc.vector.tensor_tensor(st[0:LINE, 1, :, :], s[2], s[5], ALU.add))
                        link(nc.vector.tensor_tensor(st[0:LINE, 2, :, :], st[0:LINE, 0, :, :], st[0:LINE, 0, :, :], ALU.mult))
                        link(nc.vector.scalar_tensor_tensor(out=st[0:LINE, 3, :, :], in0=st[0:LINE, 2, :, :],
                                                            scalar=C / 4.0, in1=st[0:LINE, 1, :, :],
                                                            op0=ALU.mult, op1=ALU.add))
                        nc.vector.tensor_scalar(st[0:LINE, 5 + c % 2, :, :], st[0:LINE, 3, :, :],
                                                1.0 / (C * Z_SCALE ** 2), EPS_MIX / Z_SCALE ** 2,
                                                ALU.mult, ALU.add).then_inc(s_mv, 1)

                    def lines_out(grp, c):
                        dve.wait_ge(s_sc, i * NG * NLC + grp * NLC + c + 1)
                        dve.wait_ge(s_sb, i * NG * NLC + grp * NLC + c + 1)
                        y = y_f[0:LINE, :, c * LC:(c + 1) * LC]
                        last = nc.vector.tensor_tensor(y, y, buf_b[0:LINE, :, c * LC:(c + 1) * LC], ALU.add)
                        last.then_inc(s_z, 1)

                    for k in range(NCHK):
                        v_low(k)
                    for grp in range(NG):
                        for q in range(grp * NOCT, (grp + 1) * NOCT):
                            o8 = (q % NOCT) * OCT
                            dve.wait_ge(s_yf, i * CV + q + 1)
                            b = buf_b[0:LINE, o8:o8 + OCT, :].rearrange("p c g -> p (c g)")
                            nc.vector.tensor_tensor(b, b, sv[0:LINE, q % 2, 1, :], ALU.mult).then_inc(s_yr, 1)
                        dve.wait_ge(s_yr, START + i * CV + (grp + 1) * NOCT)
                        per = LC // CH
                        for c in range(NLC + 2):
                            if c < NLC:
                                line_stats(grp, c)
                            if 1 <= c <= NLC:
                                lines_out(grp, c - 1)
                            if c >= 2 and grp < NG - 1:
                                for k in range((c - 2) * per, (c - 1) * per):
                                    v_low((grp + 1) * NCHK + k)
                    assert chain[0] == CHAIN


CHAIN_PER_CHUNK = 4
V_SCALE = H_SCALE * W_TOP
DVE_NATURAL = 5 + TAPS + 2 + 5
DVE_EVAC = DVE_NATURAL + 20
DVE_GAMMA = DVE_EVAC + 3
BU_PARTS = DVE_GAMMA + 6
DVE_CENTRED = BU_PARTS + 6 + 8 + 4
DVE_OUT = DVE_CENTRED + 5
DVE_SETUP = DVE_OUT + 4
POOL_CONSTS = 19


def experts(nc, g):
    x_v, z_rows, z_cols, out_v = g["x_v"], g["z_rows"], g["z_cols"], g["out_v"]
    ident, mean_w, mhalf, var_sel, row_sel = g["ident"], g["mean_w"], g["mhalf"], g["var_sel"], g["row_sel"]
    wout_hi, wout_lo, proj_b, scales = g["wout_hi"], g["wout_lo"], g["proj_b"], g["scales"]
    bank, pair = g["psum"], g["pairs"]
    ctx = ExitStack()
    with ctx:
        def sb(name, shape, dt=F32):
            return ctx.enter_context(nc.sbuf_tensor(name, shape, dt))

        def sem(name):
            return ctx.enter_context(nc.semaphore(name))

        x1 = sb("x1", [128, N])
        zr = sb("zr", [128, N])
        zc = sb("zc", [128, W, H])
        tok_hi = sb("tok_hi", [128, N], F16)
        tok_lo = sb("tok_lo", [128, N], F16)
        z_hi = sb("z_hi", [128, 2, TB], F16)
        z_lo = sb("z_lo", [128, 2, TB], F16)
        sq = sb("sq_b", [128, 2, TB])
        hf = sb("hf_b", [128, NHF, TB])
        vr = sb("vr_b", [RSTD_ROWS, 4, TB])
        vparts = sb("vparts_b", [RSTD_ROWS, TB], BF16)[:, :]
        rw_hi = sb("rw_hi", [128, E], F16)
        rw_lo = sb("rw_lo", [128, E], F16)
        rw = sb("rw", [128, E])
        rb_row = sb("rb_row", [1, E])
        ones_row = sb("ones_row", [1, 128])
        rb = sb("rb", [128, E])
        order = sb("order", [128, E])
        ew_hi = sb("ew_hi", [128, E, C], F16)
        ew_lo = sb("ew_lo", [128, E, C], F16)
        eb3 = sb("eb3", [3, E * C], BF16)
        pb3 = sb("pb3", [3, C], BF16)
        ones3 = sb("ones3_b", [3, TB], BF16)
        mxs = sb("largest", [128, 4])
        q = sb("largest_of_all", [1, 4])
        srow = sb("factor_row", [1, 6])
        esc = sb("expert_factors", [128, 6])
        lg = sb("lg", [128, TT, E])
        oh = sb("oh", [128, TT, E])
        l2 = sb("l2", [128, TT, E])
        gate = sb("gate", [128, TT, E])
        m1 = sb("m1", [128, TT])
        m2 = sb("m2", [128, TT])
        acc = sb("acc", [128, 2, C])
        part = sb("part", [128, 2, 4, C])
        fin = sb("fin", [128, 2, C])
        res = sb("res", [128, 2, TB])

        s_load = sem("expert_weights_loaded")
        s_pc = sem("expert_pool_constants")
        s_zr = sem("z_rows_loaded")
        s_zc = sem("z_cols_loaded")
        s_dv = sem("expert_dve_step")
        s_pe = sem("expert_pe_step")

        ew = x1[:, 0:E * C].rearrange("p (e c) -> p e c", e=E)
        neg = x1[:, 7 * E * C:8 * E * C]
        pb_row = x1[0:1, 8 * E * C:8 * E * C + C]
        pb_res = x1[0:1, 8 * E * C + C:8 * E * C + 2 * C]
        pb_part = x1[0:1, 8 * E * C + 2 * C:8 * E * C + 4 * C].bitcast(BF16)[:, 0:3 * C].rearrange("p (k n) -> p k n", k=3)
        eb_row = x1[0:1, 2 * E * C:3 * E * C]
        eb_res = x1[0:1, 3 * E * C:4 * E * C]
        eb_part = x1[0:1, 4 * E * C:6 * E * C].bitcast(BF16)[:, 0:3 * E * C].rearrange("p (k n) -> p k n", k=3)

        def load_z(sp, i):
            sp.dma_start(zr[:, :], z_rows[bass.ds(i, 1), :, :].rearrange("b c n -> (b c) n")).then_inc(s_zr, 16)
            sp.dma_start(zc[:, :, :].rearrange("p w h -> p (w h)"),
                         z_cols[bass.ds(i, 1), :, :].rearrange("b c n -> (b c) n")).then_inc(s_zc, 16)

        with nc.Block() as block:
            @block.sync
            def _(sp):
                sp.dma_start(ew, g["expert_w"].rearrange("e d c -> d e c")).then_inc(s_load, 16)
                sp.dma_start(rw[:, :], g["router_w"]).then_inc(s_load, 16)
                sp.dma_start(rb_row[:, :], g["router_b"].rearrange("(a e) -> a e", a=1)).then_inc(s_load, 16)
                sp.dma_start(eb_row, g["expert_b"].rearrange("(a e) c -> a (e c)", a=1)).then_inc(s_load, 16)
                load_z(sp, 0)
                sp.wait_ge(s_dv, BIAS_PARTS)
                for k in range(3):
                    sp.dma_start(eb3[k:k + 1, :], eb_part[:, k, :]).then_inc(s_load, 16)
                    sp.dma_start(pb3[k:k + 1, :], pb_part[:, k, :]).then_inc(s_load, 16)
                sp.wait_ge(s_load, 16 * 10)

            @block.gpsimd
            def _(pool):
                nc.gpsimd.memset(ones3[:, :], 1.0).then_inc(s_pc, 1)
                nc.gpsimd.memset(ones_row[:, :], 1.0).then_inc(s_pc, 1)
                for e in range(E):
                    nc.gpsimd.memset(order[:, e:e + 1], float(E - e)).then_inc(s_pc, 1)
                pool.wait_ge(s_pc, 2 + E)

            @block.tensor
            def _(pe):
                pe.wait_ge(s_load, 16 * 4)
                pe.wait_ge(s_pc, 2 + E)
                nc.tensor.matmul(bank[0][:, 0:E], ones_row[:, :], rb_row[:, :], start=True, stop=True)
                pe.wait_ge(s_dv, EX_NATURAL)
                nc.tensor.matmul(bank[2][0:1, 0:C], proj_b[:, :], ident[:, :], start=True, stop=True)
                for n in range(4):
                    mm = nc.tensor.matmul(bank[1][0:1, n * C:(n + 1) * C], mxs[:, n:n + 1], ident[:, :], start=True, stop=True)
                mm.then_inc(s_pe, 1)
                pe.wait_ge(s_dv, EX_FACTORS)
                nc.tensor.matmul(bank[3][:, 0:6], ones_row[:, :], srow[:, :], start=True, stop=True).then_inc(s_pe, 1)

            @block.vector
            def _(dve):
                step = [0]

                def done(ins):
                    step[0] += 1
                    ins.then_inc(s_dv, 1)
                    dve.wait_ge(s_dv, step[0])
                dve.wait_ge(s_load, 16 * 4)
                done(nc.vector.tensor_scalar(neg, x1[:, 0:E * C], -1.0, None, ALU.mult))
                done(nc.vector.tensor_reduce(mxs[:, 0:1], x1[:, 0:E * C], AX.X, ALU.max))
                done(nc.vector.tensor_reduce(mxs[:, 1:2], neg, AX.X, ALU.max))
                done(nc.vector.tensor_scalar(neg[:, 0:E], rw[:, :], -1.0, None, ALU.mult))
                done(nc.vector.tensor_reduce(mxs[:, 2:3], rw[:, :], AX.X, ALU.max))
                done(nc.vector.tensor_reduce(mxs[:, 3:4], neg[:, 0:E], AX.X, ALU.max))
                assert step[0] == EX_NATURAL
                dve.wait_ge(s_pe, 1)
                done(nc.vector.tensor_reduce(q[:, 0:1], bank[1][0:1, 0:2 * C], AX.X, ALU.max))
                done(nc.vector.tensor_reduce(q[:, 1:2], bank[1][0:1, 2 * C:4 * C], AX.X, ALU.max))
                done(nc.vector.tensor_scalar(q[:, 0:2], q[:, 0:2], TINY, None, ALU.add))
                done(nc.vector.reciprocal(q[:, 2:4], q[:, 0:2]))
                for n in range(2):
                    done(nc.vector.tensor_scalar(srow[:, 3 * n:3 * n + 1], q[:, 2 + n:3 + n], T_TOP, None, ALU.mult))
                    done(nc.vector.tensor_scalar(srow[:, 3 * n + 1:3 * n + 2], q[:, 2 + n:3 + n], T_TOP * H_SCALE, None, ALU.mult))
                    done(nc.vector.tensor_scalar(srow[:, 3 * n + 2:3 * n + 3], q[:, n:n + 1], 1.0 / (T_TOP * H_SCALE), None,
                                                 ALU.mult))
                assert step[0] == EX_FACTORS
                dve.wait_ge(s_pe, 2)
                done(nc.vector.tensor_copy(esc[:, :], bank[3][:, 0:6]))
                done(nc.vector.tensor_scalar(eb_row, eb_row, esc[0:1, 1:2], None, ALU.mult))
                done(nc.vector.tensor_scalar(pb_row, bank[2][0:1, 0:C], scales[0:1, 6:7], Z_SCALE, ALU.mult, ALU.mult))
                for row, rest, parts in ((eb_row, eb_res, eb_part), (pb_row, pb_res, pb_part)):
                    done(nc.vector.tensor_copy(parts[:, 0, :], row))
                    done(nc.vector.tensor_tensor(rest, row, parts[:, 0, :], ALU.subtract))
                    done(nc.vector.tensor_copy(parts[:, 1, :], rest))
                    done(nc.vector.tensor_tensor(row, rest, parts[:, 1, :], ALU.subtract))
                    done(nc.vector.tensor_copy(parts[:, 2, :], row))
                assert step[0] == BIAS_PARTS
                done(nc.vector.tensor_scalar(x1[:, 0:E * C], x1[:, 0:E * C], esc[:, 0:1], None, ALU.mult))
                done(nc.vector.tensor_copy(ew_hi[:, :, :], ew))
                done(nc.vector.tensor_tensor(ew_lo[:, :, :], ew, ew_hi[:, :, :], ALU.subtract))
                done(nc.vector.tensor_scalar(rw[:, :], rw[:, :], esc[:, 3:4], None, ALU.mult))
                done(nc.vector.tensor_copy(rw_hi[:, :], rw[:, :]))
                done(nc.vector.tensor_tensor(rw_lo[:, :], rw[:, :], rw_hi[:, :], ALU.subtract))
                done(nc.vector.tensor_copy(rb[:, :], bank[0][:, 0:E]))

        XL = 8
        s_x = [sem(f"residual_x_loaded_{p}") for p in range(XL)]
        s_za = sem("z_summed")
        s_zh = sem("z_high_done")
        s_zl = sem("z_low_done")
        s_pj = sem("projected")
        s_x1 = sem("x1_done")
        s_mean = sem("token_mean_done")
        s_xc = sem("token_centred")
        s_sq = sem("token_squared")
        s_var = sem("token_var_done")
        s_root = sem("token_rstd_done")
        s_inv = sem("token_inverse_variance_done")
        s_sqrt = sem("token_root_done")
        s_ln = sem("token_rstd_chain")
        s_bc = sem("token_rstd_broadcast")
        s_hf = sem("token_norm_done")
        s_th = sem("token_high_done")
        s_tl = sem("token_low_done")
        s_rt = sem("logits_done")
        s_ch = sem("gate_chain")
        s_ge = sem("gate_exponent_wanted")
        s_ex = sem("gate_exponent_done")
        s_gate = sem("gates_done")
        s_ea = sem("experts_0_3_done")
        s_eb = sem("experts_4_7_done")
        s_acc = sem("experts_0_3_gated")
        s_part = sem("experts_4_7_gated")
        s_pl = sem("pool_sum_step")
        s_fin = sem("experts_summed")
        s_gs = sem("gated_sum_step")
        s_tr = sem("sum_transposed")
        s_res = sem("result_done")
        s_st = [sem(f"result_stored_{i}") for i in range(2)]

        TPB = TT // 2
        from_one = (s_x1, s_res, s_xc, s_pj, s_var, s_hf, s_tl, s_fin, s_tr, s_st[0], s_st[1])

        with nc.Block() as block:
            @block.sync
            def _(sp):
                def load_x(i, p):
                    sp.dma_start(x1[:, p * (N // XL):(p + 1) * (N // XL)],
                                 x_v[bass.ds(i, 1), :, p * (N // XL):(p + 1) * (N // XL)].rearrange("b c n -> (b c) n")
                                 ).then_inc(s_x[p], 16)

                def store(i, n):
                    sp.dma_start(out_v[bass.ds(i, 1), :, n * TB:(n + 1) * TB].rearrange("b c n -> (b c) n"),
                                 res[:, n % 2, :]).then_inc(s_st[n % 2], 16)

                for p in range(XL):
                    load_x(0, p)
                with sp.Fori(1, B) as i:
                    sp.wait_ge(s_hf, START + i * NTB)
                    load_z(sp, i)
                    for n in range(NTB):
                        sp.wait_ge(s_res, START + i * NTB - NTB + n + 1)
                        store(i - 1, n)
                        if (n + 1) % (NTB // XL) == 0:
                            load_x(i, n // (NTB // XL))
                for n in range(NTB):
                    sp.wait_ge(s_res, START + (B - 1) * NTB + n + 1)
                    store(B - 1, n)
                for p in range(2):
                    sp.wait_ge(s_st[p], START + 16 * B * NTB // 2)

            def tb(n):
                return slice(n * TB, (n + 1) * TB)

            @block.tensor
            def _(pe):
                with pe.Fori(0, B) as i:
                    def project(n):
                        pe.wait_ge(s_zl, i * NTB + n + 1)
                        pe.wait_ge(s_x1, START + i * NTB + max(n - 1, 0))
                        if n == 0:
                            pe.wait_ge(s_res, START + i * NTB)
                        nc.tensor.matmul(bank[n % 2][:, 0:TB], pb3[:, :], ones3[:, :], start=True, stop=False)
                        for k, (a, b) in enumerate(((wout_hi, z_hi), (wout_hi, z_lo), (wout_lo, z_hi))):
                            mm = nc.tensor.matmul(bank[n % 2][:, 0:TB], a[:, :], b[:, n % 2, :], start=False, stop=(k == 2))
                        mm.then_inc(s_pj, 1)

                    def mean(n):
                        pe.wait_ge(s_x1, START + i * NTB + n + 1)
                        pe.wait_ge(s_xc, START + i * NTB + n)
                        nc.tensor.matmul(bank[2][:, 0:TB], mean_w[:, :], x1[:, tb(n)], start=True, stop=True).then_inc(s_mean, 1)

                    def var(n):
                        pe.wait_ge(s_sq, i * NTB + n + 1)
                        nc.tensor.matmul(bank[3][0:RSTD_ROWS, 0:TB], var_sel[:, 31 - n:31 - n + RSTD_ROWS], sq[:, n % 2, :],
                                         start=(n == 0), stop=(n == NTB - 1)).then_inc(s_var, 1)

                    def spread(n):
                        if n >= 2:
                            pe.wait_ge(s_hf, START + i * NTB + n - 1)
                        else:
                            pe.wait_ge(s_root, i + 1)
                        nc.tensor.matmul(bank[n % 2][:, 0:TB], row_sel[:, n:n + 1].to_broadcast([RSTD_ROWS, 128]), vparts,
                                         start=True, stop=True).then_inc(s_bc, 1)

                    for n in range(NTB + 2):
                        if n < NTB:
                            project(n)
                        if 1 <= n <= NTB:
                            mean(n - 1)
                        if n >= 2:
                            var(n - 2)
                    for n in range(NTB):
                        spread(n)

                    pe.wait_ge(s_tl, START + (i + 1) * NTB)
                    for t in range(TT):
                        ts = slice(t * 128, (t + 1) * 128)
                        o = bank[2 + t // TPB][:, (t % TPB) * E:(t % TPB + 1) * E]
                        for k, (a, b) in enumerate(((tok_hi, rw_hi), (tok_hi, rw_lo), (tok_lo, rw_hi))):
                            mm = nc.tensor.matmul(o, a[:, ts], b[:, :], start=(t % TPB == 0 and k == 0), stop=(k == 2),
                                                  skip_group_check=True)
                    mm.then_inc(s_rt, 1)

                    def expert(t):
                        ts = slice(t * 128, (t + 1) * 128)
                        for half, (free, done) in enumerate(((s_acc, s_ea), (s_part, s_eb))):
                            if t >= 2:
                                pe.wait_ge(free, i * TT + t - 1)
                            o = pair[half][:, t % 2, :]
                            es = slice(half * 4, half * 4 + 4)
                            nc.tensor.matmul(o, ones3[:, 0:128], eb3[:, half * 4 * C:(half + 1) * 4 * C], start=True, stop=False)
                            for k, (a, b) in enumerate(((tok_hi, ew_hi), (tok_hi, ew_lo), (tok_lo, ew_hi))):
                                mm = nc.tensor.matmul(o, a[:, ts], b[:, es, :].rearrange("p e c -> p (e c)"),
                                                      start=False, stop=(k == 2))
                            mm.then_inc(done, 1)

                    def turn(t):
                        pe.wait_ge(s_fin, START + i * TT + t + 1)
                        n = t // TPC
                        if t % TPC == 0:
                            if n >= 2:
                                pe.wait_ge(s_res, START + i * NTB + n - 1)
                        mm = nc.tensor.transpose(bank[n % 2][:, (t % TPC) * 128:(t % TPC + 1) * 128], fin[:, t % 2, :],
                                                 ident[:, :])
                        mm.then_inc(s_tr, 1)

                    for t in range(TT + 2):
                        if t < TT:
                            expert(t)
                        if t >= 2:
                            turn(t - 2)

            @block.scalar
            def _(act):
                with act.Fori(0, B) as i:
                    def z_high(n):
                        act.wait_ge(s_za, i * NTB + n + 1)
                        act.wait_ge(s_pj, START + i * NTB + max(n - 1, 0))
                        nc.scalar.activation(z_hi[:, n % 2, :], zr[:, tb(n)], ACT.Copy).then_inc(s_zh, 1)

                    def square(n):
                        act.wait_ge(s_xc, START + i * NTB + n + 1)
                        act.wait_ge(s_var, START + i * NTB + max(n - 1, 0))
                        nc.scalar.activation(sq[:, n % 2, :], zr[:, tb(n)], ACT.Square).then_inc(s_sq, 1)

                    def high(n):
                        act.wait_ge(s_hf, START + i * NTB + n + 1)
                        nc.scalar.activation(tok_hi[:, tb(n)], hf[:, n % NHF, :], ACT.Copy).then_inc(s_th, 1)

                    for n in range(NTB + 2):
                        if n < NTB:
                            z_high(n)
                        if n >= 2:
                            square(n - 2)
                    act.wait_ge(s_inv, i + 1)
                    nc.scalar.activation(vr[:, 2, :], vr[:, 1, :], ACT.Sqrt).then_inc(s_sqrt, 1)
                    for n in range(NTB):
                        high(n)

                    act.wait_ge(s_ge, i + 1)
                    nc.scalar.activation(gate[:, :, :], lg[:, :, :], ACT.Exp).then_inc(s_ex, 1)

                    act.wait_ge(s_gate, i + 1)
                    for t in range(TT):
                        act.wait_ge(s_eb, i * TT + t + 1)
                        act.wait_ge(s_fin, START + i * TT + max(t - 1, 0))
                        for e in range(4):
                            last = nc.scalar.activation(part[:, t % 2, e, :], pair[1][:, t % 2, e * C:(e + 1) * C], ACT.Copy,
                                                        scale=gate[:, t, 4 + e:5 + e])
                        last.then_inc(s_part, 1)

            @block.gpsimd
            def _(pool):
                for s in from_one:
                    pool.sem_inc(s, START)
                with pool.Fori(0, B) as i:
                    def z_low(n):
                        pool.wait_ge(s_zh, i * NTB + n + 1)
                        nc.gpsimd.tensor_tensor(z_lo[:, n % 2, :], zr[:, tb(n)], z_hi[:, n % 2, :], ALU.subtract
                                                ).then_inc(s_zl, 1)

                    def low(n):
                        pool.wait_ge(s_th, i * NTB + n + 1)
                        nc.gpsimd.tensor_tensor(tok_lo[:, tb(n)], hf[:, n % NHF, :], tok_hi[:, tb(n)], ALU.subtract
                                                ).then_inc(s_tl, 1)

                    for n in range(NTB):
                        z_low(n)
                    for n in range(NTB):
                        low(n)

                    for t in range(TT):
                        pool.wait_ge(s_part, i * TT + t + 1)
                        p = part[:, t % 2, :, :]
                        nc.gpsimd.tensor_tensor(p[:, 0:2, :], p[:, 0:2, :], p[:, 2:4, :], ALU.add).then_inc(s_pl, 1)
                        pool.wait_ge(s_pl, i * (2 * TT) + 2 * t + 1)
                        nc.gpsimd.tensor_tensor(p[:, 0, :], p[:, 0, :], p[:, 1, :], ALU.add).then_inc(s_pl, 1)
                        pool.wait_ge(s_pl, i * (2 * TT) + 2 * t + 2)
                        pool.wait_ge(s_acc, i * TT + t + 1)
                        pool.wait_ge(s_tr, START + i * TT + max(t - 1, 0))
                        nc.gpsimd.tensor_tensor(fin[:, t % 2, :], p[:, 0, :], acc[:, t % 2, :], ALU.add).then_inc(s_fin, 1)

            @block.vector
            def _(dve):
                with dve.Fori(0, B) as i:
                    chain = [0]

                    def link(ins):
                        chain[0] += 1
                        ins.then_inc(s_ch, 1)
                        dve.wait_ge(s_ch, i * GATE_CHAIN + chain[0])

                    def z_sum(n):
                        if n == 0:
                            dve.wait_ge(s_zr, i * 16 + 16)
                            dve.wait_ge(s_zc, i * 16 + 16)
                        rows = TB // W
                        v = zr[:, tb(n)].rearrange("p (h w) -> p h w", w=W)
                        nc.vector.tensor_tensor(v, v, zc[:, :, n * rows:(n + 1) * rows].rearrange("p w h -> p h w"), ALU.add
                                                ).then_inc(s_za, 1)

                    def residual(n):
                        dve.wait_ge(s_x[n // (NTB // XL)], i * 16 + 16)
                        dve.wait_ge(s_pj, START + i * NTB + n + 1)
                        nc.vector.scalar_tensor_tensor(out=x1[:, tb(n)], in0=bank[n % 2][:, 0:TB], scalar=scales[:, 7:8],
                                                       in1=x1[:, tb(n)], op0=ALU.mult, op1=ALU.add).then_inc(s_x1, 1)

                    def centre(n):
                        dve.wait_ge(s_mean, i * NTB + n + 1)
                        nc.vector.tensor_tensor(zr[:, tb(n)], x1[:, tb(n)], bank[2][:, 0:TB], ALU.subtract
                                                ).then_inc(s_xc, 1)

                    def normal(n):
                        dve.wait_ge(s_bc, i * NTB + n + 1)
                        dve.wait_ge(s_tl, START + i * NTB + max(n - NHF + 1, 0))
                        nc.vector.tensor_tensor(hf[:, n % NHF, :], zr[:, tb(n)], bank[n % 2][:, 0:TB], ALU.mult).then_inc(s_hf, 1)

                    for n in range(NTB + 2):
                        if n < NTB:
                            z_sum(n)
                        if 1 <= n <= NTB:
                            residual(n - 1)
                        if n >= 2:
                            centre(n - 2)
                    dve.wait_ge(s_var, START + (i + 1) * NTB)
                    rstd_rows(nc, dve, i, vr, vparts, bank[3][0:RSTD_ROWS, 0:TB], EPS_TOK, s_ln, s_inv, s_sqrt, s_root)
                    for n in range(NTB):
                        normal(n)

                    dve.wait_ge(s_rt, i + 1)
                    wide = [128, TT, E]
                    ob = order[:, :].unsqueeze(1).to_broadcast(wide)

                    def spread(t):
                        return t[:, :].unsqueeze(2).to_broadcast(wide)
                    for half in range(2):
                        ts = slice(half * TPB, (half + 1) * TPB)
                        last = nc.vector.tensor_scalar(lg[:, ts, :].rearrange("p t e -> p (t e)"),
                                                       bank[2 + half][:, 0:TPB * E], esc[:, 5:6], None, ALU.mult)
                    link(last)
                    link(nc.vector.tensor_tensor(lg[:, :, :], lg[:, :, :], rb[:, :].unsqueeze(1).to_broadcast(wide), ALU.add))

                    def first_largest(src, m, dst):
                        link(nc.vector.tensor_reduce(m[:, :], src[:, :, :], AX.X, ALU.max))
                        link(nc.vector.tensor_tensor(dst[:, :, :], src[:, :, :], spread(m), ALU.is_equal))
                        link(nc.vector.tensor_tensor(dst[:, :, :], dst[:, :, :], ob, ALU.mult))
                        link(nc.vector.tensor_reduce(m2[:, :], dst[:, :, :], AX.X, ALU.max))
                        link(nc.vector.tensor_tensor(dst[:, :, :], ob, spread(m2), ALU.is_equal))

                    first_largest(lg, m1, oh)
                    link(nc.vector.scalar_tensor_tensor(out=l2[:, :, :].rearrange("p t e -> p (t e)"),
                                                        in0=oh[:, :, :].rearrange("p t e -> p (t e)"), scalar=-1e30,
                                                        in1=lg[:, :, :].rearrange("p t e -> p (t e)"),
                                                        op0=ALU.mult, op1=ALU.add))
                    nc.vector.tensor_tensor(lg[:, :, :], lg[:, :, :], spread(m1), ALU.subtract).then_inc(s_ge, 1)
                    dve.wait_ge(s_ge, i + 1)
                    first_largest(l2, m1, l2)
                    link(nc.vector.tensor_tensor(oh[:, :, :], oh[:, :, :], l2[:, :, :], ALU.add))
                    dve.wait_ge(s_ex, i + 1)
                    link(nc.vector.tensor_tensor(gate[:, :, :], gate[:, :, :], oh[:, :, :], ALU.mult))
                    link(nc.vector.tensor_reduce(m1[:, :], gate[:, :, :], AX.X, ALU.add))
                    link(nc.vector.reciprocal(m2[:, :], m1[:, :]))
                    link(nc.vector.tensor_scalar(m2[:, :], m2[:, :], esc[:, 2:3], None, ALU.mult))
                    nc.vector.tensor_tensor(gate[:, :, :], gate[:, :, :], spread(m2), ALU.mult).then_inc(s_gate, 1)
                    dve.wait_ge(s_gate, i + 1)
                    assert chain[0] == GATE_CHAIN

                    def gated(t):
                        dve.wait_ge(s_ea, i * TT + t + 1)
                        dve.wait_ge(s_fin, START + i * TT + max(t - 1, 0))
                        a = acc[:, t % 2, :]
                        nc.vector.tensor_scalar(a, pair[0][:, t % 2, 0:C], gate[:, t, 0:1], None, ALU.mult).then_inc(s_gs, 1)
                        for e in range(1, 4):
                            dve.wait_ge(s_gs, i * (3 * TT) + 3 * t + e)
                            last = nc.vector.scalar_tensor_tensor(out=a, in0=pair[0][:, t % 2, e * C:(e + 1) * C],
                                                                  scalar=gate[:, t, e:e + 1], in1=a,
                                                                  op0=ALU.mult, op1=ALU.add)
                            last.then_inc(s_gs if e < 3 else s_acc, 1)

                    def result(n):
                        dve.wait_ge(s_tr, START + i * TT + (n + 1) * TPC)
                        dve.wait_ge(s_st[n % 2], START + i * (16 * (NTB // 2)) + 16 * (n // 2))
                        nc.vector.tensor_tensor(res[:, n % 2, :], bank[n % 2][:, 0:TB], x1[:, tb(n)], ALU.add
                                                ).then_inc(s_res, 1)

                    LAG = TPC + 3
                    for t in range(TT + LAG):
                        if t < TT:
                            gated(t)
                        if t >= LAG and (t - LAG) % TPC == 0:
                            result((t - LAG) // TPC)
                    assert (TT - 1) // TPC * TPC <= TT + LAG - 1 - LAG


EX_NATURAL = 6
EX_FACTORS = EX_NATURAL + 10
BIAS_PARTS = EX_FACTORS + 13
GATE_CHAIN = 2 + 1 + 5 + 1 + 5 + 1 + 3

_INS = ['x', 'L0_conv_W_in', 'L0_conv_b_in', 'L0_conv_dw_w', 'L0_conv_dw_b', 'L0_conv_gamma', 'L0_conv_beta',
        'L0_conv_W_out', 'L0_conv_b_out', 'L0_ffn_router_w', 'L0_ffn_router_b', 'L0_ffn_expert_w', 'L0_ffn_expert_b']


def kernel(**inputs):
    import numpy as _np
    import concourse.bacc as _bacc
    from concourse import mybir as _mybir
    from concourse.bass_utils import run_bass_kernel_spmd as _run

    nc = _bacc.Bacc("TRN2", target_bir_lowering=False, num_devices=1)
    arrays, args = {}, []
    for name in _INS:
        a = _np.ascontiguousarray(inputs[name])
        arrays[f"in_{name}"] = a
        args.append(nc.dram_tensor(f"in_{name}", a.shape, _mybir.dt.from_np(a.dtype), kind="ExternalInput").ap())
    args.append(nc.dram_tensor("out_0", (B, C, H, W), F32, kind="ExternalOutput").ap())
    build(nc, *args)
    r = _run(nc, [arrays], core_ids=[0])
    return r.results[0]["out_0"]
```
